# Optimizing a Trainium2 kernel written in Bass

```python
import numpy as np
import jax
import jax.numpy as jnp

def _softmax(x, axis=-1):
    return jax.nn.softmax(x, axis=axis)

def _gelu(x):
    return jax.nn.gelu(x, approximate=True)

def _silu(x):
    return jax.nn.silu(x)

def _sigmoid(x):
    return jax.nn.sigmoid(x)

def _layernorm(x, axis=-1, eps=1e-05):
    m = jnp.mean(x, axis=axis, keepdims=True)
    v = jnp.var(x, axis=axis, keepdims=True)
    return (x - m) / jnp.sqrt(v + eps)

def _scatter_add(tgt, idx, src, axis=0):
    return tgt.at[idx].add(src)

def _segment_sum(src, seg, n):
    return jax.ops.segment_sum(src, seg, n)
kernel_name = 'mk_hybrid_d1_jaxref_r4_f06ae2'

def setup_inputs(seed: int=0):
    np.random.seed(seed)
    _w = jnp.asarray

    def _L0_attn_a_setup():
        import jax, jax.numpy as jnp
        import numpy as np
        H = 32
        HKV = 8
        D = 1024
        HD = D // H
        S = 256
        MASK_OUT = 0.9
        MIN_REMAIN = 128
        THETA = 10000.0

        def rope_tables(seq_len, hd):
            inv_freq = 1.0 / THETA ** (jnp.arange(0, hd, 2, dtype=jnp.float32) / hd)
            t = jnp.arange(seq_len, dtype=jnp.float32)
            freqs = jnp.outer(t, inv_freq)
            emb = jnp.concatenate([freqs, freqs], axis=-1)
            return (jnp.cos(emb), jnp.sin(emb))

        def rotate_half(x):
            x1, x2 = jnp.split(x, 2, axis=-1)
            return jnp.concatenate([-x2, x1], axis=-1)

        def apply_rope(x, cos, sin):
            return x * cos + rotate_half(x) * sin
        key = jax.random.key(seed)
        k0, k1, k2, k3, k4 = jax.random.split(key, 5)
        hidden_states = jax.random.normal(k0, (1, S, D), jnp.float32)
        Wq = jax.random.normal(k1, (D, D), jnp.float32) * 0.02
        Wk = jax.random.normal(k2, (HKV * HD, D), jnp.float32) * 0.02
        Wv = jax.random.normal(k3, (HKV * HD, D), jnp.float32) * 0.02
        Wo = jax.random.normal(k4, (D, D), jnp.float32) * 0.02
        return {'hidden_states': hidden_states, 'Wq': Wq, 'Wk': Wk, 'Wv': Wv, 'Wo': Wo}
    _L0_attn_a_in = _L0_attn_a_setup()

    def _L0_attn_b_setup():
        import jax, jax.numpy as jnp
        import numpy as np
        import math
        D_MODEL = 1024
        N_HEADS = 32
        D_HEAD = D_MODEL // N_HEADS
        SEQ = 512
        BATCH = 1

        def rope(x):
            S = x.shape[2]
            D = x.shape[-1]
            theta = 1.0 / 10000.0 ** (jnp.arange(0, D, 2, dtype=jnp.float32) / D)
            ang = jnp.arange(S, dtype=jnp.float32)[:, None] * theta[None, :]
            cos = jnp.cos(ang)
            sin = jnp.sin(ang)
            x_even = x[..., ::2]
            x_odd = x[..., 1::2]
            rot_even = x_even * cos - x_odd * sin
            rot_odd = x_even * sin + x_odd * cos
            return jnp.stack((rot_even, rot_odd), axis=-1).reshape(x.shape)
        key = jax.random.key(seed)
        ks = jax.random.split(key, 9)
        scale = 1.0 / math.sqrt(D_MODEL)
        return {'x': jax.random.normal(ks[0], (BATCH, SEQ, D_MODEL), dtype=jnp.float32), 'Wq': jax.random.normal(ks[1], (D_MODEL, D_MODEL), dtype=jnp.float32) * scale, 'bq': jnp.zeros((D_MODEL,), dtype=jnp.float32), 'Wk': jax.random.normal(ks[2], (D_MODEL, D_MODEL), dtype=jnp.float32) * scale, 'bk': jnp.zeros((D_MODEL,), dtype=jnp.float32), 'Wv': jax.random.normal(ks[3], (D_MODEL, D_MODEL), dtype=jnp.float32) * scale, 'bv': jnp.zeros((D_MODEL,), dtype=jnp.float32), 'Wo': jax.random.normal(ks[4], (D_MODEL, D_MODEL), dtype=jnp.float32) * scale, 'bo': jnp.zeros((D_MODEL,), dtype=jnp.float32)}
    _L0_attn_b_in = _L0_attn_b_setup()

    def _L0_ffn_setup():
        import jax, jax.numpy as jnp
        import numpy as np
        B, S, IN, OUT = (4, 512, 1024, 1024)
        E, K, R = (8, 2, 16)
        CAP_FACTOR = 3.0
        ALPHA = 1.0 / R
        LN_EPS = 1e-05
        key = jax.random.key(seed)
        ks = jax.random.split(key, 6)
        return {'x': jax.random.normal(ks[0], (B, S, IN), dtype=jnp.float32), 'weight': jax.random.normal(ks[1], (OUT, IN), dtype=jnp.float32) * 0.02, 'lora_A': jax.random.normal(ks[2], (E, IN, R), dtype=jnp.float32) / np.sqrt(R), 'lora_B': jax.random.normal(ks[3], (E, R, OUT), dtype=jnp.float32) * 0.02, 'gw1': jax.random.normal(ks[4], (4 * E, IN), dtype=jnp.float32) * 0.02, 'gb1': jnp.zeros((4 * E,), dtype=jnp.float32), 'ln_gamma': jnp.ones((4 * E,), dtype=jnp.float32), 'ln_beta': jnp.zeros((4 * E,), dtype=jnp.float32), 'gw2': jax.random.normal(ks[5], (E, 4 * E), dtype=jnp.float32) * 0.02, 'gb2': jnp.zeros((E,), dtype=jnp.float32)}
    _L0_ffn_in = _L0_ffn_setup()
    _d = {'L0_attn_a_hidden_states': _L0_attn_a_in['hidden_states'], 'L0_attn_a_Wq': _L0_attn_a_in['Wq'], 'L0_attn_a_Wk': _L0_attn_a_in['Wk'], 'L0_attn_a_Wv': _L0_attn_a_in['Wv'], 'L0_attn_a_Wo': _L0_attn_a_in['Wo'], 'L0_attn_b_Wq': _L0_attn_b_in['Wq'], 'L0_attn_b_bq': _L0_attn_b_in['bq'], 'L0_attn_b_Wk': _L0_attn_b_in['Wk'], 'L0_attn_b_bk': _L0_attn_b_in['bk'], 'L0_attn_b_Wv': _L0_attn_b_in['Wv'], 'L0_attn_b_bv': _L0_attn_b_in['bv'], 'L0_attn_b_Wo': _L0_attn_b_in['Wo'], 'L0_attn_b_bo': _L0_attn_b_in['bo'], 'L0_ffn_weight': _L0_ffn_in['weight'], 'L0_ffn_lora_A': _L0_ffn_in['lora_A'], 'L0_ffn_lora_B': _L0_ffn_in['lora_B'], 'L0_ffn_gw1': _L0_ffn_in['gw1'], 'L0_ffn_gb1': _L0_ffn_in['gb1'], 'L0_ffn_ln_gamma': _L0_ffn_in['ln_gamma'], 'L0_ffn_ln_beta': _L0_ffn_in['ln_beta'], 'L0_ffn_gw2': _L0_ffn_in['gw2'], 'L0_ffn_gb2': _L0_ffn_in['gb2']}
    _x0 = _d['L0_attn_a_hidden_states']
    _d['L0_attn_a_hidden_states'] = jax.random.normal(jax.random.fold_in(jax.random.key(seed), 1), (2, 1024, 1024), dtype=_x0.dtype)
    del _x0
    return _d

def reference(L0_attn_a_hidden_states, L0_attn_a_Wq, L0_attn_a_Wk, L0_attn_a_Wv, L0_attn_a_Wo, L0_attn_b_Wq, L0_attn_b_bq, L0_attn_b_Wk, L0_attn_b_bk, L0_attn_b_Wv, L0_attn_b_bv, L0_attn_b_Wo, L0_attn_b_bo, L0_ffn_weight, L0_ffn_lora_A, L0_ffn_lora_B, L0_ffn_gw1, L0_ffn_gb1, L0_ffn_ln_gamma, L0_ffn_ln_beta, L0_ffn_gw2, L0_ffn_gb2):

    def _L0_attn_a_ref(hidden_states, Wq, Wk, Wv, Wo):
        import jax, jax.numpy as jnp
        import numpy as np
        H = 32
        HKV = 8
        D = 1024
        HD = D // H
        S = 256
        MASK_OUT = 0.9
        MIN_REMAIN = 128
        THETA = 10000.0

        def rope_tables(seq_len, hd):
            inv_freq = 1.0 / THETA ** (jnp.arange(0, hd, 2, dtype=jnp.float32) / hd)
            t = jnp.arange(seq_len, dtype=jnp.float32)
            freqs = jnp.outer(t, inv_freq)
            emb = jnp.concatenate([freqs, freqs], axis=-1)
            return (jnp.cos(emb), jnp.sin(emb))

        def rotate_half(x):
            x1, x2 = jnp.split(x, 2, axis=-1)
            return jnp.concatenate([-x2, x1], axis=-1)

        def apply_rope(x, cos, sin):
            return x * cos + rotate_half(x) * sin
        B, Sq, Dm = hidden_states.shape
        dtype = hidden_states.dtype
        neg = jnp.finfo(dtype).min
        q = (hidden_states @ Wq.T).reshape(B, Sq, H, HD).transpose(0, 2, 1, 3)
        k = (hidden_states @ Wk.T).reshape(B, Sq, HKV, HD).transpose(0, 2, 1, 3)
        v = (hidden_states @ Wv.T).reshape(B, Sq, HKV, HD).transpose(0, 2, 1, 3)
        rep = H // HKV
        k = jnp.repeat(k, rep, axis=1)
        v = jnp.repeat(v, rep, axis=1)
        cos, sin = rope_tables(Sq, HD)
        qr = apply_rope(q, cos, sin)
        kr = apply_rope(k, cos, sin)
        draft = jnp.einsum('bhqd,bhkd->bhqk', qr, kr)
        qi = jnp.arange(Sq)
        ki = jnp.arange(Sq)
        causal_future = qi[:, None] < ki[None, :]
        draft = draft + jnp.where(causal_future, neg, jnp.asarray(0.0, dtype))
        num_remain = max(min(Sq, MIN_REMAIN), Sq - int(Sq * MASK_OUT))
        _, draft_indices = jax.lax.top_k(draft, num_remain)
        mask = jnp.full((B, H, Sq, Sq), neg, dtype)
        b_idx = jnp.arange(B)[:, None, None, None]
        h_idx = jnp.arange(H)[None, :, None, None]
        s_idx = jnp.arange(Sq)[None, None, :, None]
        mask = mask.at[b_idx, h_idx, s_idx, draft_indices].set(0.0)
        mask = jnp.where(causal_future[None, None, :, :], neg, mask)
        scores = jnp.einsum('bhqd,bhkd->bhqk', qr, kr) / np.sqrt(HD).astype(np.float32) + mask
        attn = jax.nn.softmax(scores, axis=-1)
        out = jnp.einsum('bhqk,bhkd->bhqd', attn, v)
        out = out.transpose(0, 2, 1, 3).reshape(B, Sq, Dm)
        return out @ Wo.T

    def _L0_attn_b_ref(x, Wq, bq, Wk, bk, Wv, bv, Wo, bo):
        import jax, jax.numpy as jnp
        import numpy as np
        import math
        D_MODEL = 1024
        N_HEADS = 32
        D_HEAD = D_MODEL // N_HEADS
        SEQ = 512
        BATCH = 1

        def rope(x):
            S = x.shape[2]
            D = x.shape[-1]
            theta = 1.0 / 10000.0 ** (jnp.arange(0, D, 2, dtype=jnp.float32) / D)
            ang = jnp.arange(S, dtype=jnp.float32)[:, None] * theta[None, :]
            cos = jnp.cos(ang)
            sin = jnp.sin(ang)
            x_even = x[..., ::2]
            x_odd = x[..., 1::2]
            rot_even = x_even * cos - x_odd * sin
            rot_odd = x_even * sin + x_odd * cos
            return jnp.stack((rot_even, rot_odd), axis=-1).reshape(x.shape)
        B, S, _ = x.shape

        def proj(W, b):
            h = x @ W.T + b
            return h.reshape(B, S, N_HEADS, D_HEAD).transpose(0, 2, 1, 3)
        Q = rope(proj(Wq, bq))
        K = rope(proj(Wk, bk))
        V = proj(Wv, bv)
        scores = jnp.einsum('bhqd,bhkd->bhqk', Q, K) / math.sqrt(D_HEAD)
        causal = jnp.tril(jnp.ones((S, S), dtype=bool))
        scores = jnp.where(causal[None, None], scores, jnp.float32(-jnp.inf))
        attn = jax.nn.softmax(scores, axis=-1)
        out = jnp.einsum('bhqk,bhkd->bhqd', attn, V)
        out = out.transpose(0, 2, 1, 3).reshape(B, S, N_HEADS * D_HEAD)
        return out @ Wo.T + bo

    def _L0_ffn_ref(x, weight, lora_A, lora_B, gw1, gb1, ln_gamma, ln_beta, gw2, gb2):
        import jax, jax.numpy as jnp
        import numpy as np
        B, S, IN, OUT = (4, 512, 1024, 1024)
        E, K, R = (8, 2, 16)
        CAP_FACTOR = 3.0
        ALPHA = 1.0 / R
        LN_EPS = 1e-05
        orig_shape = x.shape
        xf = x.reshape(-1, orig_shape[-1])
        N = xf.shape[0]
        capacity = int(CAP_FACTOR * N / E)
        h = xf @ gw1.T + gb1
        mu = jnp.mean(h, axis=-1, keepdims=True)
        var = jnp.mean((h - mu) ** 2, axis=-1, keepdims=True)
        h = (h - mu) * jax.lax.rsqrt(var + LN_EPS) * ln_gamma + ln_beta
        h = jax.nn.relu(h)
        gates = h @ gw2.T + gb2
        top_v, top_i = jax.lax.top_k(gates, K)
        top_g = jax.nn.softmax(top_v, axis=-1)
        onehot = (top_i[..., None] == jnp.arange(E)).astype(xf.dtype)
        counts = onehot.sum(axis=0)
        allowed = (counts <= capacity).astype(xf.dtype)
        w = jnp.einsum('nke,nk,ke->ne', onehot, top_g, allowed)
        main = xf @ weight.T
        tmp = jnp.einsum('ni,eir->enr', xf, lora_A)
        tmp = tmp * w.T[:, :, None]
        lora = jnp.einsum('enr,ero->no', tmp, lora_B) * ALPHA
        out = main + lora
        return out.reshape(*orig_shape[:-1], weight.shape[0])
    x = L0_attn_a_hidden_states
    x = x + _L0_attn_a_ref(_layernorm(x, axis=-1), L0_attn_a_Wq, L0_attn_a_Wk, L0_attn_a_Wv, L0_attn_a_Wo)
    x = x + _L0_ffn_ref(_layernorm(x, axis=-1), L0_ffn_weight, L0_ffn_lora_A, L0_ffn_lora_B, L0_ffn_gw1, L0_ffn_gb1, L0_ffn_ln_gamma, L0_ffn_ln_beta, L0_ffn_gw2, L0_ffn_gb2)
    x = x + _L0_attn_b_ref(_layernorm(x, axis=-1), L0_attn_b_Wq, L0_attn_b_bq, L0_attn_b_Wk, L0_attn_b_bk, L0_attn_b_Wv, L0_attn_b_bv, L0_attn_b_Wo, L0_attn_b_bo)
    x = x + _L0_ffn_ref(_layernorm(x, axis=-1), L0_ffn_weight, L0_ffn_lora_A, L0_ffn_lora_B, L0_ffn_gw1, L0_ffn_gb1, L0_ffn_ln_gamma, L0_ffn_ln_beta, L0_ffn_gw2, L0_ffn_gb2)
    return x

_drawn_inputs = setup_inputs


def setup_inputs(seed=0):
    import zlib

    import numpy as np

    out = dict(_drawn_inputs(seed))
    spreads = {'L0_attn_b_bq': (0.0, 0.8),
     'L0_attn_b_bk': (0.0, 0.8),
     'L0_attn_b_bv': (0.0, 0.1),
     'L0_attn_b_bo': (0.0, 0.1),
     'L0_ffn_gb1': (0.0, 0.8),
     'L0_ffn_ln_gamma': (1.0, 0.6),
     'L0_ffn_ln_beta': (0.0, 0.8),
     'L0_ffn_gb2': (0.0, 0.307)}
    factors = {'L0_ffn_lora_A': 3.001, 'L0_ffn_lora_B': 2.983, 'L0_ffn_gw1': 3.42, 'L0_ffn_gw2': 3.515}
    for name, (base, spread) in spreads.items():
        noise = np.random.default_rng([zlib.crc32(name.encode()), seed]).standard_normal(out[name].shape)
        drawn = base * np.exp(spread * noise) if base else spread * noise
        out[name] = jnp.asarray(drawn.astype(out[name].dtype))
    for name, factor in factors.items():
        out[name] = (out[name] * factor).astype(out[name].dtype)
    return out
```

```python
from contextlib import ExitStack

import numpy as np

import concourse.bass as bass
from concourse import mybir

F32 = mybir.dt.float32
BF16 = mybir.dt.bfloat16
U32 = mybir.dt.uint32
ALU = mybir.AluOpType
ACT = mybir.ActivationFunctionType

P = 128
BATCH, SEQ, DM = 2, 1024, 1024
NH, HD = 32, 32
HG = P // HD
NG = NH // HG
NT = SEQ // P
KT = DM // P
NTOK = BATCH * NT
TOP = 128
E, R = 8, 16
HID = 4 * E
CAPACITY = int(3.0 * BATCH * SEQ / E)
LN_EPS = 1e-5

QK_SCALE = 2.0 ** -30
EXP_SCALE = (1.0 / (QK_SCALE * QK_SCALE)) / float(np.sqrt(np.float32(HD)))
FUTURE = -0.25
TAKEN = -1.0

TR_LN = 2 * NT
TR_UNIT = [HG * -(-(i + 1) // 4) + 1 for i in range(NT)]
TR_GROUP = sum(TR_UNIT)
TR_WO = 2 * KT
TR_BATCH = TR_LN + NG * TR_GROUP + TR_WO
PJ_GROUP = 14
QK_ROPE = {"half": [(d + 16) % 32 for d in range(32)], "pairs": [d ^ 1 for d in range(32)]}


class Tally:

    def __init__(self, sem, credit=0):
        self.sem, self.base, self.n, self.credit = sem, 0, 0, credit

    def at(self, base):
        self.base, self.n = base, 0

    def mark(self, ins):
        ins.then_inc(self.sem, 1)
        self.n += 1
        return self.n

    def reached(self, eng, n=None):
        eng.wait_ge(self.sem, self.base + ((self.n if n is None else n) + self.credit))



def build(nc, I, rope_cos, rope_sin, ident_d, future_d, iota_d, x1, x2, x3, out):
    ctx = ExitStack()
    with ctx:
        def sb(name, shape, dt=F32):
            return ctx.enter_context(nc.sbuf_tensor(name, shape, dt))

        def sem(name):
            return ctx.enter_context(nc.semaphore(name))

        ident = sb("ident", [P, P])
        ident16 = sb("ident16", [P, P], BF16)
        future16 = sb("future16", [P, P], BF16)
        ones = sb("ones", [P, P])
        iota = sb("iota", [P, E])
        arena = sb("arena", [P, 52736])

        S_ring = ctx.enter_context(nc.psum_tensor("S_ring", [P, 2, 1024], F32))
        TR_ring = ctx.enter_context(nc.psum_tensor("TR_ring", [P, 2, 512], F32))
        PJ = ctx.enter_context(nc.psum_tensor("PJ", [P, 512], F32))
        PV = ctx.enter_context(nc.psum_tensor("PV", [P, 512], F32))

        def carve():
            at = [0]

            def take(*dims):
                n = int(np.prod(dims))
                a = arena[:, at[0]:at[0] + n]
                at[0] += n
                assert at[0] <= 52736, at[0]
                if len(dims) == 2:
                    a = a.rearrange("p (a b) -> p a b", a=dims[0])
                if len(dims) == 3:
                    a = a.rearrange("p (a b c) -> p a b c", a=dims[0], b=dims[1])
                return a
            return take

        take = carve()
        XT = take(KT, SEQ)
        OT = take(NG, SEQ)
        XL = OT
        W_stage = take(3, DM)
        bo_row = W_stage[0:1, 0, :]
        WT = take(KT, P)
        NXT = take(3, SEQ)
        SH = take(2, SEQ)
        NXV = take(NT, P)
        CUR_QK = take(2, SEQ)
        CUR_V = take(NT, P)
        S_sb = take(2, HG, SEQ)
        WoT = arena[:, 0:0]
        SEL = take(HG, SEQ)
        EX = take(HG, SEQ)
        PT = take(HG * NT, P)
        COS = take(SEQ)
        SIN = take(SEQ)
        small = take(512)
        m8 = small[:, 0:32].rearrange("p (h e) -> p h e", h=HG)
        m8b = small[:, 32:64].rearrange("p (h e) -> p h e", h=HG)
        nb = small[:, 64:68]
        sums = small[:, 68:72]
        rinv = small[:, 384:512]
        bias_st = small[:, 76:79]
        ln_st = small[:, 80:92].rearrange("p (a b) -> p a b", a=2)
        ln_mv = small[:, 96:128].rearrange("p (t c) -> p t c", c=2)
        ln_ve = small[:, 128:144]
        ln_sd = small[:, 144:160]
        ln_r = small[:, 160:176]
        ln_t = small[:, 176:192]
        Rsb = small[:, 256:384]

        s0 = dict(const=sem("const"), ones=sem("ones"), apart=sem("apart"))

        dma = dict(xl=[sem(f"xl{t}") for t in range(NT)], wo=[sem(f"wo{k}") for k in range(4)],
                              xo=[sem(f"xo{k}") for k in range(4)], st=[sem(f"st{k}") for k in range(4)],
                              fx=[sem(f"fx{k}") for k in range(4)], fw=[sem(f"fw{k}") for k in range(4)])

        def layer_sems(L):
            s = dict(**{n: sem(f"{L}_{n}") for n in (
                      "tab", "x_norm", "ln_var", "ln_sd", "tr_full", "tr_free", "pj_full", "pj_free", "s_full",
                      "s_free", "s_copied", "e_ready", "p_ready", "nb_ready", "rinv_ready", "pv_full", "pv_free",
                      "handoff", "shuffled", "roped", "o_full", "o_free", "chain", "bo")})
            s["xl"], s["wo"], s["xo"], s["st"] = dma["xl"], dma["wo"], dma["xo"], dma["st"]
            s["xl0"], s["slot0"] = (0, 0) if L == "A" else (BATCH * 16, BATCH * 32)
            s["w"] = [sem(f"{L}_w{m}") for m in range(3)]
            s["w_free"] = [sem(f"{L}_wfree{m}") for m in range(3)]
            return s

        def layer(L, topk, src, dst, rope):
            pre = "L0_attn_a_" if L == "A" else "L0_attn_b_"
            return dict(
                s=layer_sems(L), topk=topk, src=src, dst=dst, rope=rope, bias=(L == "B"), gqa=(L == "A"),
                Wq=I[pre + "Wq"], Wk=I[pre + "Wk"], Wv=I[pre + "Wv"], Wo=I[pre + "Wo"],
                b=[I[pre + n] for n in ("bq", "bk", "bv")] if L == "B" else None,
                cos=rope_cos[0 if L == "A" else 1], sin=rope_sin[0 if L == "A" else 1])

        x_in = I["L0_attn_a_hidden_states"].rearrange("b s d -> (b s) d")
        out2 = out.rearrange("b s d -> (b s) d")
        A = layer("A", True, x_in, x1, "half")
        B = layer("B", False, x2, x3, "pairs")

        PIECES = [(kind, m, k) for m in range(3) for kind in ("wt", "mm") for k in range(2)] + [("vt", 2, 0), ("vt", 2, 1)]
        assert len(PIECES) == PJ_GROUP

        def apart(eng):
            eng.sem_inc(s0["apart"], 1)

        def att_sync(sp, L):
            s = L["s"]
            sp.dma_start(COS, L["cos"]).then_inc(s["tab"], 16)
            sp.dma_start(SIN, L["sin"]).then_inc(s["tab"], 16)

            def weights(p, g):
                for m, w in enumerate((L["Wq"], L["Wk"], L["Wv"])):
                    sp.wait_ge(s["w_free"][m], p + 1)
                    apart(sp)
                    if L["gqa"] and m:
                        for c in range(HG):
                            sp.dma_start(W_stage[HD * c:HD * c + HD, m, :],
                                         w[bass.ds(g * HD, HD), :]).then_inc(s["w"][m], 16)
                    else:
                        sp.dma_start(W_stage[:, m, :], w[bass.ds(g * P, P), :]).then_inc(s["w"][m], 16)
                    if L["bias"]:
                        bias = L["b"][m].rearrange("(n o) -> n o", o=1)
                        sp.dma_start(bias_st[:, m:m + 1], bias[bass.ds(g * P, P), :]).then_inc(s["w"][m], 16)

            with sp.Fori(0, BATCH) as b:
                for t in range(NT):
                    sp.dma_start(XL[:, t, :], L["src"][bass.ds(b * SEQ + t * P, P), :]).then_inc(s["xl"][t], 16)
                with sp.Fori(0, NG) as g:
                    weights(b * NG + g, g)
                if L["bias"]:
                    sp.wait_ge(s["w_free"][0], (b + 1) * NG + 1)
                    apart(sp)
                    sp.dma_start(bo_row, I["L0_attn_b_bo"].rearrange("(a n) -> a n", a=1)).then_inc(s["bo"], 16)
                sp.wait_ge(s["rinv_ready"], (b + 1) * (NG * NT))
                apart(sp)
                for ro in range(KT):
                    if ro >= 4:
                        sp.wait_ge(s["tr_full"], b * TR_BATCH + (TR_LN + NG * TR_GROUP + 2 * (ro - 3)))
                        apart(sp)
                    sp.dma_start(SEL[:, ro % 4, :], L["Wo"][ro * P:ro * P + P, :]).then_inc(s["wo"][ro % 4], 16)
                sp.wait_ge(s["pv_full"], (b + 1) * (NG * NT))
                apart(sp)
                for t in range(NT + 4):
                    if t >= 4:
                        sp.wait_ge(s["o_free"], b * NT + (t - 4) + 1 + 2)
                        apart(sp)
                        sp.dma_start(L["dst"][bass.ds(b * SEQ + (t - 4) * P, P), :],
                                     EX[:, t % 4, :]).then_inc(s["st"][t % 4], 16)
                    if t < NT:
                        if t >= 4:
                            sp.wait_ge(s["st"][t % 4], b * 32 + (s["slot0"] + 16))
                            apart(sp)
                        sp.dma_start(EX[:, t % 4, :], L["src"][bass.ds(b * SEQ + t * P, P), :]).then_inc(s["xo"][t % 4], 16)
                for k in range(4):
                    sp.wait_ge(s["st"][k], b * 32 + (s["slot0"] + 32))
                    apart(sp)

        def att_tensor(pe, L):
            s = L["s"]
            tr, pj = Tally(s["tr_full"]), Tally(s["pj_full"])
            first = [True]

            def tr_slot():
                pe.wait_ge(s["tr_free"], tr.base + (tr.n + 1))
                return TR_ring[:, tr.n % 2, :]

            def piece(p, kind, m, k):
                pe.wait_ge(s["pj_free"], pj.base + (pj.n + 1))
                if kind == "wt":
                    if k == 0:
                        pe.wait_ge(s["w"][m], (p + 1) * (16 * ((HG if L["gqa"] and m else 1) + (1 if L["bias"] else 0))))
                    for c in range(4):
                        ins = pe.transpose(PJ[:, c * P:c * P + P], W_stage[:, m, (4 * k + c) * P:(4 * k + c + 1) * P],
                                           ident[:, :])
                        if m and k == 0 and c == 0:
                            ins.then_inc(s["w_free"][m - 1], 1)
                    pj.mark(ins)
                elif kind == "mm":
                    for kt in range(KT):
                        ins = pe.matmul(PJ[:, :], WT[:, kt, :], XT[:, kt, k * 512:k * 512 + 512],
                                        start=(kt == 0), stop=(kt == KT - 1))
                    pj.mark(ins)
                else:
                    for c in range(4):
                        t = 4 * k + c
                        ins = pe.transpose(PJ[:, c * P:c * P + P], NXT[:, 2, t * P:t * P + P], ident[:, :])
                        if t == 0:
                            ins.then_inc(s["w_free"][2], 1)
                    pj.mark(ins)

            def scores(it, i):
                n = (i + 1) * P
                for h in range(HG):
                    x = i * HG + h
                    pe.wait_ge(s["s_free"], it * (NT * HG) + (x + 1))
                    q = CUR_QK[HD * h:HD * h + HD, 0, i * P:i * P + P]
                    for c in range(0, n, 512):
                        w = min(512, n - c)
                        last = c + w == n
                        pe.matmul(S_ring[:, x % 2, c:c + w], q, CUR_QK[HD * h:HD * h + HD, 1, c:c + w],
                                  start=True, stop=not last)
                    pe.matmul(S_ring[:, x % 2, n - P:n], ident16[:, :], future16[:, :],
                              start=False, stop=True).then_inc(s["s_full"], 1)

            def attention(it, g, project):
                pe.wait_ge(s["handoff"], it * 3 + 3)
                scores(it, 0)
                for i in range(NT):
                    if i + 1 < NT:
                        scores(it, i + 1)
                        if project:
                            for j in (2 * i, 2 * i + 1):
                                piece(it + 1, *PIECES[j])
                    for h in range(HG):
                        if L["topk"] and i:
                            pe.wait_ge(s["p_ready"], it * (HG * (NT - 1)) + ((i - 1) * HG + h + 1))
                        else:
                            pe.wait_ge(s["e_ready"], it * (HG * NT) + (i * HG + h + 1))
                        for c in range(0, i + 1, 4):
                            slot = tr_slot()
                            for kt in range(c, min(c + 4, i + 1)):
                                ins = pe.transpose(slot[:, (kt - c) * P:(kt - c + 1) * P],
                                                   EX[:, h, kt * P:kt * P + P], ident[:, :])
                            tr.mark(ins)
                    pe.wait_ge(s["tr_free"], tr.base + (tr.n + 2))
                    pe.wait_ge(s["pv_free"], it * NT + (i + 1))
                    for h in range(HG):
                        for kt in range(i + 1):
                            ins = pe.matmul(PV[HD * h:HD * h + HD, 0:P], CUR_V[:, kt, HD * h:HD * h + HD],
                                            PT[:, h * NT + kt, :], start=(kt == 0), stop=(kt == i))
                    ins.then_inc(s["pv_full"], 1)
                    slot = tr_slot()
                    pe.wait_ge(s["rinv_ready"], it * NT + (i + 1))
                    tr.mark(pe.matmul(slot[:, 0:P], rinv, ident[:, :],
                                        start=True, stop=True))

            with pe.Fori(0, BATCH) as b:
                tr.at(b * TR_BATCH)
                pj.at(b * (PJ_GROUP * NG))
                for t in range(NT):
                    pe.wait_ge(s["x_norm"], b * NT + (t + 1))
                    for k in range(2):
                        slot = tr_slot()
                        for c in range(4):
                            ins = pe.transpose(slot[:, c * P:c * P + P], XL[:, t, (4 * k + c) * P:(4 * k + c + 1) * P],
                                               ident[:, :])
                        tr.mark(ins)
                pe.wait_ge(s["tr_free"], tr.base + (tr.n + 2))
                pe.wait_ge(s["o_free"], b * NT + 2)
                for q in PIECES:
                    piece(b * NG, *q)
                with pe.Fori(0, NG - 1) as g:
                    tr.at(b * TR_BATCH + TR_LN + g * TR_GROUP)
                    pj.at(b * (PJ_GROUP * NG) + PJ_GROUP + g * PJ_GROUP)
                    attention(b * NG + g, g, True)
                    assert tr.n == TR_GROUP and pj.n == PJ_GROUP
                tr.at(b * TR_BATCH + TR_LN + (NG - 1) * TR_GROUP)
                attention(b * NG + NG - 1, NG - 1, False)
                WoT = S_sb.rearrange("p a h n -> p (a h) n")
                for ro in range(KT):
                    pe.wait_ge(s["wo"][ro % 4], b * 32 + (s["slot0"] + 16 + 16 * (ro // 4)))
                    for k in range(2):
                        slot = tr_slot()
                        for c in range(4):
                            ins = pe.transpose(slot[:, c * P:c * P + P], SEL[:, ro % 4, (4 * k + c) * P:(4 * k + c + 1) * P],
                                               ident[:, :])
                        tr.mark(ins)
                pe.wait_ge(s["tr_free"], tr.base + (tr.n + 2))
                pe.wait_ge(s["s_free"], (b + 1) * (NG * NT * HG) + 2)
                pe.wait_ge(s["pv_free"], (b + 1) * (NG * NT) + 1)
                if L["bias"]:
                    pe.wait_ge(s["bo"], b * 16 + 16)
                for t in range(NT):
                    pe.wait_ge(s["o_free"], b * NT + (t + 1))
                    for c in range(2):
                        for kt in range(KT):
                            ins = pe.matmul(S_ring[:, t % 2, c * 512:c * 512 + 512], OT[:, kt, t * P:t * P + P],
                                            WoT[:, kt, c * 512:c * 512 + 512], start=(kt == 0),
                                            stop=(kt == KT - 1 and not L["bias"]))
                        if L["bias"]:
                            ins = pe.matmul(S_ring[:, t % 2, c * 512:c * 512 + 512], ones[0:1, :],
                                            bo_row[0:1, c * 512:c * 512 + 512], start=False, stop=True)
                    ins.then_inc(s["o_full"], 1)
                assert True

        def att_scalar(act, L):
            s = L["s"]
            tr, pj = Tally(s["tr_free"]), Tally(s["pj_free"])
            act.sem_inc(s["s_free"], 2)
            act.sem_inc(s["tr_free"], 2)
            act.sem_inc(s["pj_free"], 1)

            def tr_out(dst, cols=512, split=4):
                act.wait_ge(s["tr_full"], tr.base + (tr.n + 1))
                src = TR_ring[:, tr.n % 2, 0:cols]
                if split:
                    src = src.rearrange("p (c n) -> p c n", n=P)
                tr.mark(act.copy(dst, src))

            def piece(kind, m, k):
                act.wait_ge(s["pj_full"], pj.base + (pj.n + 1))
                if kind == "wt":
                    pj.mark(act.copy(WT[:, 4 * k:4 * k + 4, :], PJ[:, :].rearrange("p (c n) -> p c n", n=P)))
                elif kind == "mm":
                    dst = NXT[:, m, k * 512:k * 512 + 512]
                    if L["bias"]:
                        pj.mark(act.activation(dst, PJ[:, :], ACT.Identity, bias=bias_st[:, m:m + 1]))
                    else:
                        pj.mark(act.copy(dst, PJ[:, :]))
                else:
                    pj.mark(act.copy(NXV[:, 4 * k:4 * k + 4, :], PJ[:, :].rearrange("p (c n) -> p c n", n=P)))

            def scores_out(it, i):
                if i >= 2:
                    act.wait_ge(s["rinv_ready"], it * NT + (i - 1))
                n = (i + 1) * P
                for h in range(HG):
                    x = i * HG + h
                    act.wait_ge(s["s_full"], it * (NT * HG) + (x + 1))
                    act.copy(S_sb[:, i % 2, h, 0:n], S_ring[:, x % 2, 0:n]).then_inc(s["s_free"], 1)

            def attention(it, project):
                act.wait_ge(s["handoff"], it * 3 + 3)
                scores_out(it, 0)
                for i in range(NT):
                    n = (i + 1) * P
                    if i + 1 < NT:
                        scores_out(it, i + 1)
                        if project:
                            for j in (2 * i, 2 * i + 1):
                                piece(*PIECES[j])
                    act.wait_ge(s["nb_ready"], it * NT + (i + 1))
                    act.wait_ge(s["s_free"], it * (NT * HG) + (i * HG + HG + 2))
                    for h in range(HG):
                        if L["topk"] and i:
                            ins = act.activation(EX[:, h, 0:n], S_sb[:, i % 2, h, 0:n], ACT.Exp,
                                                 bias=nb[:, h:h + 1], scale=EXP_SCALE)
                        else:
                            ins = act.activation(EX[:, h, 0:n], S_sb[:, i % 2, h, 0:n], ACT.Exp,
                                                 bias=nb[:, h:h + 1], scale=EXP_SCALE, accum_out=sums[:, h:h + 1])
                        ins.then_inc(s["e_ready"], 1)
                    for h in range(HG):
                        for c in range(0, i + 1, 4):
                            w = min(4, i + 1 - c)
                            tr_out(PT[:, h * NT + c:h * NT + c + w, :], cols=w * P)
                    tr_out(Rsb, cols=P, split=0)

            with act.Fori(0, BATCH) as b:
                tr.at(b * TR_BATCH)
                pj.at(b * (PJ_GROUP * NG))
                act.wait_ge(s["ln_var"], b + 1)
                act.activation(ln_sd[:, 0:NT], ln_ve[:, 0:NT], ACT.Sqrt).then_inc(s["ln_sd"], 1)
                for t in range(NT):
                    for k in range(2):
                        tr_out(XT[:, 4 * k:4 * k + 4, t * P:t * P + P])
                for q in PIECES:
                    piece(*q)
                with act.Fori(0, NG - 1) as g:
                    tr.at(b * TR_BATCH + TR_LN + g * TR_GROUP)
                    pj.at(b * (PJ_GROUP * NG) + PJ_GROUP + g * PJ_GROUP)
                    attention(b * NG + g, True)
                tr.at(b * TR_BATCH + TR_LN + (NG - 1) * TR_GROUP)
                attention(b * NG + NG - 1, False)
                WoT = S_sb.rearrange("p a h n -> p (a h) n")
                for ro in range(KT):
                    for k in range(2):
                        tr_out(WoT[:, 4 * k:4 * k + 4, ro * P:ro * P + P])
                assert tr.n == TR_GROUP + TR_WO

        def layer_norm(dve, s, chain, n_tiles, b1, load_wait, tile, eps_to_act, write):
            for t in range(n_tiles):
                load_wait(t)
                x = tile(t)
                if t:
                    chain.reached(dve)
                chain.mark(dve.bn_stats(ln_st[:, 0, :], x[:, 0:512]))
                chain.mark(dve.bn_stats(ln_st[:, 1, :], x[:, 512:1024]))
                chain.reached(dve)
                apart(dve)
                chain.mark(dve.bn_aggr(ln_mv[:, t, :], ln_st))
            chain.reached(dve)
            dve.tensor_scalar(ln_ve[:, 0:n_tiles], ln_mv[:, 0:n_tiles, 1], LN_EPS, None, ALU.add).then_inc(s["ln_var"], 1)
            dve.wait_ge(s["ln_sd"], b1)
            r, tt, ve = ln_r[:, 0:n_tiles], ln_t[:, 0:n_tiles], ln_ve[:, 0:n_tiles]
            chain.mark(dve.reciprocal(r, ln_sd[:, 0:n_tiles]))
            chain.reached(dve)
            chain.mark(dve.tensor_tensor(tt, ve, r, ALU.mult))
            chain.reached(dve)
            chain.mark(dve.tensor_tensor(tt, tt, r, ALU.mult))
            chain.reached(dve)
            chain.mark(dve.tensor_scalar(tt, tt, -0.5, 1.5, ALU.mult, ALU.add))
            chain.reached(dve)
            chain.mark(dve.tensor_tensor(r, r, tt, ALU.mult))
            chain.reached(dve)
            if write is not None:
                for t in range(n_tiles):
                    write(t)

        CH_LN = 3 * NT + 5
        CH_GROUP = {True: (NT - 1) * (HG * 32 + 1) + 1 * HG + 1, False: NT * HG + 1}

        def att_vector(dve, L):
            s = L["s"]
            ch = Tally(s["chain"])
            per_group = {True: (NT - 1) * HG * 32 + HG, False: NT * HG}[L["topk"]]
            per_batch = CH_LN + NG * per_group
            dve.sem_inc(s["pv_free"], 1)
            dve.sem_inc(s["o_free"], 2)
            for m in range(3):
                dve.sem_inc(s["w_free"][m], 1)

            def finalize(it, g, i):
                dve.wait_ge(s["pv_full"], it * NT + (i + 1))
                dve.wait_ge(s["tr_free"], ch_tr[0] + (sum(TR_UNIT[:i + 1]) + 2))
                dve.tensor_tensor(OT[:, g, i * P:i * P + P], PV[:, 0:P], Rsb, ALU.mult).then_inc(s["pv_free"], 1)

            def shuffle(p1, m):
                dve.wait_ge(s["pj_free"], p1 * PJ_GROUP + (4 * m + 4 + 1))
                apart(dve)
                dve.stream_shuffle(SH[:, m, :], NXT[:, m, :], QK_ROPE[L["rope"]]).then_inc(s["shuffled"], 1)

            ch_tr = [0]

            def attention(it, b, g, project):
                ch_tr[0] = b * TR_BATCH + TR_LN + g * TR_GROUP
                dve.wait_ge(s["roped"], it * 2 + 2)
                dve.wait_ge(s["pj_free"], it * PJ_GROUP + (PJ_GROUP + 1))
                for m in range(2):
                    dve.tensor_tensor(CUR_QK[:, m, :], NXT[:, m, :], SH[:, m, :], ALU.add).then_inc(s["handoff"], 1)
                dve.tensor_copy(CUR_V, NXV).then_inc(s["handoff"], 1)
                for i in range(NT):
                    n = (i + 1) * P
                    sel = L["topk"] and i > 0
                    last = [0] * HG
                    if ch.n:
                        ch.reached(dve)
                    for h in range(HG):
                        dve.wait_ge(s["s_free"], it * (NT * HG) + (i * HG + h + 1 + 2))
                        apart(dve)
                        last[h] = ch.mark(dve.max(m8[:, h, :], S_sb[:, i % 2, h, 0:n]))
                    if sel:
                        for r in range(TOP // 8):
                            for h in range(HG):
                                top = m8[:, h, :] if r == 0 else m8b[:, h, :]
                                ch.reached(dve, last[h])
                                apart(dve)
                                last[h] = ch.mark(dve.match_replace(
                                    SEL[:, h, 0:n], top, S_sb[:, i % 2, h, 0:n] if r == 0 else SEL[:, h, 0:n], TAKEN))
                            if r + 1 < TOP // 8:
                                for h in range(HG):
                                    ch.reached(dve, last[h])
                                    apart(dve)
                                    last[h] = ch.mark(dve.max(m8b[:, h, :], SEL[:, h, 0:n]))
                    ch.reached(dve)
                    dve.tensor_scalar(nb[:, :], m8[:, :, 0], -EXP_SCALE, None, ALU.mult).then_inc(s["nb_ready"], 1)
                    if i:
                        finalize(it, g, i - 1)
                    if project and i == 2:
                        shuffle(it + 1, 0)
                    if project and i == 4:
                        shuffle(it + 1, 1)
                    for h in range(HG) if sel else (HG - 1,):
                        dve.wait_ge(s["e_ready"], it * (HG * NT) + (i * HG + h + 1))
                        if sel:
                            dve.scalar_tensor_tensor(out=EX[:, h, 0:n], in0=SEL[:, h, 0:n], scalar=TAKEN / 2,
                                                     in1=EX[:, h, 0:n], op0=ALU.is_le, op1=ALU.mult,
                                                     accum_out=sums[:, h:h + 1]).then_inc(s["p_ready"], 1)
                    if sel:
                        dve.wait_ge(s["p_ready"], it * (HG * (NT - 1)) + i * HG)
                    dve.reciprocal(rinv.rearrange("p (h d) -> p h d", h=HG),
                                   sums.unsqueeze(2).to_broadcast([P, HG, HD])).then_inc(s["rinv_ready"], 1)
                finalize(it, g, NT - 1)

            with dve.Fori(0, BATCH) as b:
                ch.at(b * per_batch)

                def norm(t):
                    dve.tensor_scalar(XL[:, t, :], XL[:, t, :], ln_mv[:, t, 0:1], ln_r[:, t:t + 1], ALU.subtract,
                                      ALU.mult).then_inc(s["x_norm"], 1)

                layer_norm(dve, s, ch, NT, b + 1, lambda t: dve.wait_ge(s["xl"][t], b * 16 + (s["xl0"] + 16)), lambda t: XL[:, t, :],
                           None, norm)
                assert ch.n == CH_LN, ch.n
                for m in range(2):
                    shuffle(b * NG, m)
                with dve.Fori(0, NG - 1) as g:
                    ch.at(b * per_batch + CH_LN + g * per_group)
                    attention(b * NG + g, b, g, True)
                    assert ch.n == per_group_real(L, ch.n, per_group), (ch.n, per_group)
                ch.at(b * per_batch + CH_LN + (NG - 1) * per_group)
                attention(b * NG + NG - 1, b, NG - 1, False)
                for t in range(NT):
                    dve.wait_ge(s["o_full"], b * NT + (t + 1))
                    dve.wait_ge(s["xo"][t % 4], b * 32 + (s["slot0"] + 16 + 16 * (t // 4)))
                    dve.tensor_tensor(EX[:, t % 4, :], EX[:, t % 4, :], S_ring[:, t % 2, :],
                                      ALU.add).then_inc(s["o_free"], 1)

        def per_group_real(L, n, want):
            assert n == want, (n, want)
            return want

        def att_pool(pool, L):
            s = L["s"]

            def rope(p1):
                for m in range(2):
                    pool.wait_ge(s["shuffled"], p1 * 2 + (m + 1))
                    pool.tensor_tensor(SH[:, m, :], SH[:, m, :], SIN, ALU.mult)
                    pool.tensor_tensor(NXT[:, m, :], NXT[:, m, :], COS, ALU.mult).then_inc(s["roped"], 1)

            pool.wait_ge(s["tab"], 32)
            with pool.Fori(0, BATCH) as b:
                with pool.Fori(0, NG) as g:
                    rope(b * NG + g)

        take = carve()
        FX = take(NTOK, DM)
        NCOL = DM + HID + E * R
        FW = take(KT, NCOL)
        F_stage = take(4, DM)
        F_gw1 = take(DM)
        F_B = take(DM)
        F_xn = take(2, DM)
        F_xT = take(2, KT, P)
        F_tmp = take(NTOK, P)
        F_h = take(NTOK, HID)
        F_h2 = take(NTOK, HID)
        F_hT = take(NTOK, P)
        F_tT = F_hT
        F_g = take(NTOK, E)
        F_top = take(NTOK, E)
        F_idx = take(NTOK, E)
        F_oh = take(NTOK, 2, E)
        F_w = take(NTOK, E)
        F_w2 = take(NTOK, E)
        F_cnt = take(2 * E)
        F_p = take(NTOK, 4)
        F_mu = take(NTOK)
        F_va = take(NTOK)
        F_vb = take(NTOK)
        F_row = take(4, HID)
        F_gw2T = take(E)
        fsmall = take(512)
        f_st = fsmall[:, 0:12].rearrange("p (a b) -> p a b", a=2)
        f_mv = fsmall[:, 16:48].rearrange("p (t c) -> p t c", c=2)
        f_ve, f_sd, f_r, f_t = (fsmall[:, 64 + 16 * k:80 + 16 * k] for k in range(4))

        def ffn_layer(n, src, dst):
            s = dict(**{q: sem(f"F{n}_{q}") for q in (
                      "ln_var", "ln_sd", "x_norm", "tr_full", "tr_free", "m_full", "m_free", "a_full", "a_free", "w2",
                      "h_ln", "h_sd", "chain", "h_ready", "gates", "exp_in", "exp_out", "oh", "cnt", "t_ready", "l_full",
                      "l_done", "st", "loraA", "gw1", "misc", "h_in")})
            s["x"], s["wl"] = dma["fx"], dma["fw"]
            s["x0"], s["wl0"] = (0, 0) if n == 1 else (64, 32)
            return dict(s=s, src=src, dst=dst)

        F1 = ffn_layer(1, x1, x2)
        F2 = ffn_layer(2, x3, out2)
        FPRE = "L0_ffn_"

        def ffn_sync(sp, F):
            s = F["s"]
            for k in range(4):
                for t in range(4 * k, 4 * k + 4):
                    sp.dma_start(FX[:, t, :], F["src"][t * P:t * P + P, :]).then_inc(s["x"][k], 16)
            for ro in range(KT):
                if ro >= 4:
                    sp.wait_ge(s["tr_full"], 2 * (ro - 3))
                sp.dma_start(F_stage[:, ro % 4, :], I[FPRE + "weight"][ro * P:ro * P + P, :]).then_inc(s["wl"][ro % 4], 16)
            sp.dma_start(F_gw1[0:HID, :], I[FPRE + "gw1"]).then_inc(s["gw1"], 16)
            for e in range(E):
                for kt in range(KT):
                    sp.dma_start(FW[:, kt, DM + HID + e * R:DM + HID + e * R + R],
                                 I[FPRE + "lora_A"][e, kt * P:kt * P + P, :]).then_inc(s["loraA"], 16)
            sp.dma_start(F_B, I[FPRE + "lora_B"].rearrange("e r o -> (e r) o")).then_inc(s["misc"], 16)
            for k, nme in enumerate(("gb1", "ln_gamma", "ln_beta", "gb2")):
                w = HID if k < 3 else E
                sp.dma_start(F_row[:, k, 0:w], I[FPRE + nme].partition_broadcast(P)).then_inc(s["misc"], 16)
            sp.dma_start(F_gw2T[0:HID, :], I[FPRE + "gw2"].rearrange("e f -> f e"),
                         allow_slow_non_contiguous=True).then_inc(s["misc"], 16)
            for t in range(NTOK):
                sp.wait_ge(s["l_done"], t + 1)
                sp.dma_start(F["dst"][t * P:t * P + P, :], FX[:, t, :]).then_inc(s["st"], 16)
            sp.wait_ge(s["st"], 16 * NTOK)

        N_MISC = 6
        T_W = 2 * KT + 2

        def ffn_tensor(pe, F):
            s = F["s"]
            tr = Tally(s["tr_full"])

            def tr_slot():
                pe.wait_ge(s["tr_free"], tr.base + (tr.n + 1))
                return TR_ring[:, tr.n % 2, :]

            for ro in range(KT):
                pe.wait_ge(s["wl"][ro % 4], s["wl0"] + 16 * (1 + ro // 4))
                for k in range(2):
                    slot = tr_slot()
                    for c in range(4):
                        ins = pe.transpose(slot[:, c * P:c * P + P],
                                           F_stage[:, ro % 4, (4 * k + c) * P:(4 * k + c + 1) * P], ident[:, :])
                    tr.mark(ins)
            pe.wait_ge(s["gw1"], 16)
            for k in range(2):
                slot = tr_slot()
                for c in range(4):
                    kt = 4 * k + c
                    ins = pe.transpose(slot[:, c * HID:c * HID + HID], F_gw1[0:HID, kt * P:kt * P + P],
                                       ident[0:HID, 0:HID])
                tr.mark(ins)
            pe.wait_ge(s["tr_free"], tr.base + (tr.n + 2))
            pe.wait_ge(s["loraA"], 16 * E * KT)
            with pe.Fori(0, NTOK // 2) as tp:
                tr.at(tp * 4 + T_W)
                for q in range(2):
                    pe.wait_ge(s["x_norm"], tp * 2 + (q + 1))
                    for k in range(2):
                        slot = tr_slot()
                        for c in range(4):
                            ins = pe.transpose(slot[:, c * P:c * P + P], F_xn[:, q, (4 * k + c) * P:(4 * k + c + 1) * P],
                                               ident[:, :])
                        tr.mark(ins)
                    pe.wait_ge(s["tr_free"], tr.base + (tr.n + 2))
                    pe.wait_ge(s["m_free"], tp * 2 + (q + 1))
                    pe.wait_ge(s["a_free"], tp * 2 + (q + 1))
                    aux = (PJ, PV)[q]
                    for kt in range(KT):
                        for c in range(2):
                            ins = pe.matmul(S_ring[:, q, c * 512:c * 512 + 512], F_xT[:, q, kt, :],
                                            FW[:, kt, c * 512:c * 512 + 512], start=(kt == 0), stop=(kt == KT - 1))
                        if kt == KT - 1:
                            ins.then_inc(s["m_full"], 1)
                        ins = pe.matmul(aux[:, 0:HID + E * R], F_xT[:, q, kt, :], FW[:, kt, DM:NCOL],
                                        start=(kt == 0), stop=(kt == KT - 1))
                    ins.then_inc(s["a_full"], 1)
            tr.at(4 * (NTOK // 2) + T_W)
            pe.wait_ge(s["h_ready"], 1)
            for c in range(4):
                slot = tr_slot()
                for t in range(4 * c, 4 * c + 4):
                    ins = pe.transpose(slot[0:HID, (t % 4) * P:(t % 4 + 1) * P], F_h[:, t, :], ident[:, :])
                tr.mark(ins)
            pe.wait_ge(s["tr_free"], tr.base + (tr.n + 2))
            pe.wait_ge(s["misc"], 16 * N_MISC)
            pe.wait_ge(s["a_free"], NTOK + 2)
            for t in range(NTOK):
                ins = pe.matmul(PJ[:, t * E:t * E + E], F_hT[0:HID, t, :], F_gw2T[0:HID, :], start=True, stop=True)
            ins.then_inc(s["gates"], 1)
            pe.wait_ge(s["oh"], 1)
            for t in range(NTOK):
                ins = pe.matmul(PV[:, 0:2 * E], ones[:, :], F_oh[:, t, :, :].rearrange("p k e -> p (k e)"),
                                start=(t == 0), stop=(t == NTOK - 1))
            ins.then_inc(s["cnt"], 1)
            pe.wait_ge(s["t_ready"], 1)
            for c in range(4):
                slot = tr_slot()
                for t in range(4 * c, 4 * c + 4):
                    ins = pe.transpose(slot[:, (t % 4) * P:(t % 4 + 1) * P], F_tmp[:, t, :], ident[:, :])
                tr.mark(ins)
            pe.wait_ge(s["m_free"], NTOK + 2)
            for t in range(NTOK):
                if t % 4 == 0:
                    pe.wait_ge(s["tr_free"], tr.base + (tr.n - 4 + t // 4 + 1 + 2))
                if t >= 2:
                    pe.wait_ge(s["l_done"], t - 1)
                for c in range(2):
                    ins = pe.matmul(S_ring[:, t % 2, c * 512:c * 512 + 512], F_tT[:, t, :],
                                    F_B[:, c * 512:c * 512 + 512], start=True, stop=True)
                ins.then_inc(s["l_full"], 1)

        def ffn_scalar(act, F):
            s = F["s"]
            tr = Tally(s["tr_free"])
            act.sem_inc(s["tr_free"], 2)
            act.sem_inc(s["a_free"], 2)

            def tr_out(dst, cols=512, parts=P, n=P):
                act.wait_ge(s["tr_full"], tr.base + (tr.n + 1))
                tr.mark(act.copy(dst, TR_ring[0:parts, tr.n % 2, 0:cols].rearrange("p (c n) -> p c n", n=n)))

            for ro in range(KT):
                for k in range(2):
                    tr_out(FW[:, 4 * k:4 * k + 4, ro * P:ro * P + P])
            for k in range(2):
                tr_out(FW[:, 4 * k:4 * k + 4, DM:DM + HID], cols=4 * HID, n=HID)
            act.wait_ge(s["ln_var"], 1)
            act.activation(f_sd, f_ve, ACT.Sqrt).then_inc(s["ln_sd"], 1)
            with act.Fori(0, NTOK // 2) as tp:
                tr.at(tp * 4 + T_W)
                for q in range(2):
                    for k in range(2):
                        act.wait_ge(s["tr_full"], tr.base + (tr.n + 1))
                        tr.mark(act.copy(F_xT[:, q, 4 * k:4 * k + 4, :],
                                           TR_ring[:, tr.n % 2, :].rearrange("p (c n) -> p c n", n=P)))
                    aux = (PJ, PV)[q]
                    act.wait_ge(s["a_full"], tp * 2 + (q + 1))
                    act.copy(F_h[:, tp * 2 + q, :], aux[:, 0:HID]).then_inc(s["h_in"], 1)
                    act.copy(F_tmp[:, tp * 2 + q, :], aux[:, HID:HID + E * R]).then_inc(s["a_free"], 1)
            tr.at(4 * (NTOK // 2) + T_W)

            def tr_out2(dst, parts=P):
                act.wait_ge(s["tr_full"], tr.base + (tr.n + 1))
                tr.mark(act.copy(dst, TR_ring[0:parts, tr.n % 2, :].rearrange("p (c n) -> p c n", n=P)))

            act.wait_ge(s["h_ln"], 1)
            act.activation(F_vb, F_va, ACT.Sqrt).then_inc(s["h_sd"], 1)
            for c in range(4):
                tr_out2(F_hT[0:HID, 4 * c:4 * c + 4, :], parts=HID)
            act.wait_ge(s["exp_in"], 1)
            act.activation(F_p[:, :, 1], F_p[:, :, 0], ACT.Exp).then_inc(s["exp_out"], 1)
            for c in range(4):
                tr_out2(F_tT[:, 4 * c:4 * c + 4, :])

        def ffn_vector(dve, F):
            s = F["s"]
            ch = Tally(s["chain"])
            dve.sem_inc(s["m_free"], 2)

            def step(ins):
                ch.mark(ins)
                ch.reached(dve)

            for t in range(NTOK):
                if t % 4 == 0:
                    dve.wait_ge(s["x"][t // 4], s["x0"] + 64)
                if t:
                    ch.reached(dve)
                ch.mark(dve.bn_stats(f_st[:, 0, :], FX[:, t, 0:512]))
                step(dve.bn_stats(f_st[:, 1, :], FX[:, t, 512:1024]))
                ch.mark(dve.bn_aggr(f_mv[:, t, :], f_st))
            ch.reached(dve)
            dve.tensor_scalar(f_ve, f_mv[:, :, 1], LN_EPS, None, ALU.add).then_inc(s["ln_var"], 1)

            def inv_sqrt(r, sd, ve, tt):
                step(dve.reciprocal(r, sd))
                step(dve.tensor_tensor(tt, ve, r, ALU.mult))
                step(dve.tensor_tensor(tt, tt, r, ALU.mult))
                step(dve.tensor_scalar(tt, tt, -0.5, 1.5, ALU.mult, ALU.add))
                step(dve.tensor_tensor(r, r, tt, ALU.mult))

            dve.wait_ge(s["ln_sd"], 1)
            inv_sqrt(f_r, f_sd, f_ve, f_t)

            def norm(t, q):
                dve.tensor_scalar(F_xn[:, q, :], FX[:, t, :], f_mv[:, bass.ds(t, 1), 0], f_r[:, bass.ds(t, 1)],
                                  ALU.subtract, ALU.mult).then_inc(s["x_norm"], 1)

            norm(0, 0)
            norm(1, 1)
            CT = ch.n
            for tp in range(NTOK // 2):
                for q in range(2):
                    t = 2 * tp + q
                    dve.wait_ge(s["m_full"], t + 1)
                    if t + 2 < NTOK:
                        norm(t + 2, q)
                    dve.tensor_tensor(FX[:, t, :], FX[:, t, :], S_ring[:, q, :], ALU.add).then_inc(s["m_free"], 1)

            dve.wait_ge(s["h_in"], NTOK)
            dve.wait_ge(s["misc"], 16 * N_MISC)

            def row(k, w=HID):
                return F_row[:, k, 0:w].unsqueeze(1).to_broadcast([P, NTOK, w])

            def col(a, w):
                return a.unsqueeze(2).to_broadcast([P, NTOK, w])

            step(dve.tensor_tensor(F_h, F_h, row(0), ALU.add))
            step(dve.tensor_reduce(F_mu, F_h, mybir.AxisListType.X, ALU.add))
            step(dve.tensor_scalar(F_mu, F_mu, 1.0 / HID, None, ALU.mult))
            step(dve.tensor_tensor(F_h, F_h, col(F_mu, HID), ALU.subtract))
            step(dve.tensor_tensor(F_h2, F_h, F_h, ALU.mult))
            step(dve.tensor_reduce(F_va, F_h2, mybir.AxisListType.X, ALU.add))
            dve.tensor_scalar(F_va, F_va, 1.0 / HID, LN_EPS, ALU.mult, ALU.add).then_inc(s["h_ln"], 1)
            dve.wait_ge(s["h_sd"], 1)
            inv_sqrt(F_mu, F_vb, F_va, F_p[:, :, 0])
            step(dve.tensor_tensor(F_h, F_h, col(F_mu, HID), ALU.mult))
            step(dve.tensor_tensor(F_h, F_h, row(1), ALU.mult))
            step(dve.tensor_tensor(F_h, F_h, row(2), ALU.add))
            dve.tensor_scalar(F_h, F_h, 0.0, None, ALU.max).then_inc(s["h_ready"], 1)
            dve.wait_ge(s["gates"], 1)
            step(dve.tensor_tensor(F_g, PJ[:, 0:NTOK * E].rearrange("p (t e) -> p t e", e=E), row(3, E), ALU.add))
            for t in range(NTOK):
                ch.mark(dve.max(F_top[:, t, :], F_g[:, t, :]))
            ch.reached(dve)
            for t in range(NTOK):
                ch.mark(dve.max_index(F_idx[:, t, :].bitcast(U32), F_top[:, t, :], F_g[:, t, :]))
            ch.reached(dve)
            step(dve.tensor_copy(F_w2, F_idx.bitcast(U32)))
            for k in range(2):
                ch.mark(dve.tensor_tensor(F_oh[:, :, k, :], iota[:, :].unsqueeze(1).to_broadcast([P, NTOK, E]),
                                            col(F_w2[:, :, k], E), ALU.is_equal))
            ch.reached(dve)
            dve.tensor_tensor(F_p[:, :, 0], F_top[:, :, 1], F_top[:, :, 0], ALU.subtract).then_inc(s["exp_in"], 1)
            dve.drain().then_inc(s["oh"], 1)
            dve.wait_ge(s["exp_out"], 1)
            step(dve.tensor_scalar(F_p[:, :, 2], F_p[:, :, 1], 1.0, None, ALU.add))
            step(dve.reciprocal(F_p[:, :, 3], F_p[:, :, 2]))
            step(dve.tensor_scalar(F_p[:, :, 2], F_p[:, :, 3], 1.0 / R, None, ALU.mult))
            step(dve.tensor_tensor(F_p[:, :, 3], F_p[:, :, 2], F_p[:, :, 1], ALU.mult))
            dve.wait_ge(s["cnt"], 1)
            step(dve.tensor_scalar(F_cnt, PV[:, 0:2 * E], float(CAPACITY), None, ALU.is_le))
            for k, dst in enumerate((F_w, F_w2)):
                allowed = F_cnt[:, k * E:k * E + E].unsqueeze(1).to_broadcast([P, NTOK, E])
                step(dve.tensor_tensor(dst, F_oh[:, :, k, :], allowed, ALU.mult))
                step(dve.tensor_tensor(dst, dst, col(F_p[:, :, 2 + k], E), ALU.mult))
            step(dve.tensor_tensor(F_w, F_w, F_w2, ALU.add))
            tmp = F_tmp.rearrange("p t (e r) -> p (t e) r", r=R)
            w = F_w.rearrange("p t e -> p (t e)").unsqueeze(2).to_broadcast([P, NTOK * E, R])
            dve.wait_ge(s["a_free"], NTOK + 2)
            dve.tensor_tensor(tmp, tmp, w, ALU.mult).then_inc(s["t_ready"], 1)
            for t in range(NTOK):
                dve.wait_ge(s["l_full"], t + 1)
                dve.tensor_tensor(FX[:, t, :], FX[:, t, :], S_ring[:, t % 2, :], ALU.add).then_inc(s["l_done"], 1)

        block = ctx.enter_context(nc.Block())

        @block.sync
        def _(sp):
            sp.dma_start(ident[:, :], ident_d).then_inc(s0["const"], 16)
            sp.dma_start(ones[:, :], future_d).then_inc(s0["const"], 16)
            sp.dma_start(iota[:, :], iota_d).then_inc(s0["const"], 16)
            att_sync(sp, A)
            ffn_sync(sp, F1)
            att_sync(sp, B)
            ffn_sync(sp, F2)

        @block.tensor
        def _(pe):
            pe.wait_ge(s0["const"], 48)
            pe.wait_ge(s0["ones"], 3)
            att_tensor(pe, A)
            ffn_tensor(pe, F1)
            att_tensor(pe, B)
            ffn_tensor(pe, F2)

        @block.scalar
        def _(act):
            att_scalar(act, A)
            ffn_scalar(act, F1)
            att_scalar(act, B)
            ffn_scalar(act, F2)

        @block.vector
        def _(dve):
            dve.wait_ge(s0["const"], 48)
            dve.tensor_copy(ident16[:, :], ident[:, :]).then_inc(s0["ones"], 1)
            dve.tensor_copy(future16[:, :], ones[:, :]).then_inc(s0["ones"], 1)
            dve.wait_ge(s0["ones"], 2)
            dve.memset(ones[:, :], 1.0).then_inc(s0["ones"], 1)
            att_vector(dve, A)
            ffn_vector(dve, F1)
            att_vector(dve, B)
            ffn_vector(dve, F2)

        @block.gpsimd
        def _(pool):
            att_pool(pool, A)
            att_pool(pool, B)


_INS = ["L0_attn_a_hidden_states", "L0_attn_a_Wq", "L0_attn_a_Wk", "L0_attn_a_Wv", "L0_attn_a_Wo",
        "L0_attn_b_Wq", "L0_attn_b_bq", "L0_attn_b_Wk", "L0_attn_b_bk", "L0_attn_b_Wv", "L0_attn_b_bv",
        "L0_attn_b_Wo", "L0_attn_b_bo", "L0_ffn_weight", "L0_ffn_lora_A", "L0_ffn_lora_B", "L0_ffn_gw1",
        "L0_ffn_gb1", "L0_ffn_ln_gamma", "L0_ffn_ln_beta", "L0_ffn_gw2", "L0_ffn_gb2"]


def tables():
    pos = np.arange(SEQ, dtype=np.float32)
    inv = (1.0 / np.power(np.float32(10000.0), np.arange(0, HD, 2, dtype=np.float32) / np.float32(HD))).astype(np.float32)
    ang = (pos[None, :] * inv[:, None]).astype(np.float32)
    cos, sin = np.cos(ang).astype(np.float32), np.sin(ang).astype(np.float32)
    d = np.arange(HD)
    half, pairs = d % (HD // 2), d // 2
    sign_half = np.where(d < HD // 2, -1.0, 1.0).astype(np.float32)
    sign_pairs = np.where(d % 2 == 0, -1.0, 1.0).astype(np.float32)
    c = np.stack([np.tile(cos[half], (HG, 1)), np.tile(cos[pairs], (HG, 1))])
    s = np.stack([np.tile(sin[half] * sign_half[:, None], (HG, 1)), np.tile(sin[pairs] * sign_pairs[:, None], (HG, 1))])
    k = np.float32(QK_SCALE)
    future = np.where(np.arange(P)[None, :] > np.arange(P)[:, None], FUTURE, 0.0)
    return {
        "rope_cos": (c * k).astype(np.float32), "rope_sin": (s * k).astype(np.float32),
        "ident": np.eye(P, dtype=np.float32),
        "future": future.astype(np.float32),
        "expert_ids": np.tile(np.arange(E, dtype=np.float32), (P, 1)),
    }


def kernel(**inputs):
    import numpy as _np
    import concourse.bacc as _bacc
    from concourse import mybir as _mybir
    from concourse.bass_utils import run_bass_kernel_spmd as _run

    nc = _bacc.Bacc("TRN2", target_bir_lowering=False, num_devices=1)
    arrays, named = {}, {}
    for name in _INS:
        a = _np.ascontiguousarray(inputs[name])
        arrays[f"in_{name}"] = a
        named[name] = nc.dram_tensor(f"in_{name}", a.shape, _mybir.dt.from_np(a.dtype), kind="ExternalInput").ap()
    consts = []
    for name, a in tables().items():
        arrays[f"const_{name}"] = a
        consts.append(nc.dram_tensor(f"const_{name}", a.shape, _mybir.dt.from_np(a.dtype), kind="ExternalInput").ap())
    scratch = [nc.dram_tensor(f"x{k}", (BATCH * SEQ, DM), _mybir.dt.float32, kind="Internal").ap() for k in (1, 2, 3)]
    out = nc.dram_tensor("out", (BATCH, SEQ, DM), _mybir.dt.float32, kind="ExternalOutput").ap()
    build(nc, named, *consts, *scratch, out)
    r = _run(nc, [arrays], core_ids=[0])
    return r.results[0]["out"]
```

```python
from contextlib import ExitStack

import numpy as np

import concourse.bass as bass
from concourse import mybir

F32 = mybir.dt.float32
BF16 = mybir.dt.bfloat16
U32 = mybir.dt.uint32
I32 = mybir.dt.int32
ALU = mybir.AluOpType
ACT = mybir.ActivationFunctionType

P = 128
BATCH, SEQ, DM = 2, 1024, 1024
NH, HD = 32, 32
HG = P // HD
NG = NH // HG
NT = SEQ // P
KT = DM // P
NTOK = BATCH * NT
TOP = 128
E, R = 8, 16
HID = 4 * E
CAPACITY = int(3.0 * BATCH * SEQ / E)
LN_EPS = 1e-5

QK_SCALE = 2.0 ** -20
EXP_SCALE = (1.0 / (QK_SCALE * QK_SCALE)) / float(np.sqrt(np.float32(HD)))
FUTURE = -0.25
TAKEN = -1.0

TR_LN = 2 * NT
TR_UNIT = [HG * -(-(i + 1) // 4) + 1 for i in range(NT)]
TR_GROUP = sum(TR_UNIT)
TR_WO = 2 * KT
TR_BATCH = TR_LN + NG * TR_GROUP + TR_WO
PJ_GROUP = 14

NC = 5
CMIN = TOP - 7
AIM = (CMIN + TOP) / 2.0
STEP_OVER = 2.0
ACT_HEADS = (2, 3)
UNIT_PIECES = [(0, 1, 2), (3, 4, 5), (6,), (7, 8, 9), (10,), (11,), (12, 13), ()]
QK_ROPE = {"half": [(d + 16) % 32 for d in range(32)], "pairs": [d ^ 1 for d in range(32)]}


class Tally:

    def __init__(self, sem, credit=0):
        self.sem, self.base, self.n, self.credit = sem, 0, 0, credit

    def at(self, base):
        self.base, self.n = base, 0

    def mark(self, ins):
        ins.then_inc(self.sem, 1)
        self.n += 1
        return self.n

    def reached(self, eng, n=None):
        eng.wait_ge(self.sem, self.base + ((self.n if n is None else n) + self.credit))



def build(nc, I, rope_cos, rope_sin, ident_d, future_d, iota_d, search_d, x1, x2, x3, out):
    ctx = ExitStack()
    with ctx:
        def sb(name, shape, dt=F32):
            return ctx.enter_context(nc.sbuf_tensor(name, shape, dt))

        def sem(name):
            return ctx.enter_context(nc.semaphore(name))

        ident = sb("ident", [P, P])
        ident16 = sb("ident16", [P, P], BF16)
        future16 = sb("future16", [P, P], BF16)
        ones = sb("ones", [P, P])
        iota = sb("iota", [P, E])
        halves = sb("halves", [P, HG])
        half, one_half = halves[:, 0:1], halves[:, :]
        arena = sb("arena", [P, 52736])

        S_ring = ctx.enter_context(nc.psum_tensor("S_ring", [P, 2, 1024], F32))
        TR_ring = ctx.enter_context(nc.psum_tensor("TR_ring", [P, 2, 512], F32))
        PJ = ctx.enter_context(nc.psum_tensor("PJ", [P, 512], F32))
        PV = ctx.enter_context(nc.psum_tensor("PV", [P, 512], F32))

        def carve():
            at = [0]

            def take(*dims):
                n = int(np.prod(dims))
                a = arena[:, at[0]:at[0] + n]
                at[0] += n
                assert at[0] <= 52736, at[0]
                if len(dims) == 2:
                    a = a.rearrange("p (a b) -> p a b", a=dims[0])
                if len(dims) == 3:
                    a = a.rearrange("p (a b c) -> p a b c", a=dims[0], b=dims[1])
                return a
            return take

        take = carve()
        XT = take(KT, SEQ)
        OT = take(NG, SEQ)
        XL = OT
        W_stage = take(3, DM)
        bo_row = W_stage[0:1, 0, :]
        WT = take(KT, P)
        NXT = take(3, SEQ)
        SH = take(2, SEQ)
        NXV = take(NT, P)
        CUR_QK = take(2, SEQ)
        CUR_V = take(NT, P)
        S_sb = take(2, HG, SEQ)
        SEL = take(HG, SEQ)
        EX = take(HG, SEQ)
        PT = take(HG * NT, P)
        COS = take(SEQ)
        SIN = take(SEQ)
        small = take(512)
        G = small[:, 0:40].rearrange("p (h e) -> p h e", h=HG)
        points = small[:, 40:64].rearrange("p (s h e) -> p s h e", s=3, h=HG)
        tstar = small[:, 64:68]
        sums = small[:, 68:76].rearrange("p (s h) -> p s h", s=2)
        bias_st = small[:, 76:79]
        ended_well = small[:, 79:80].bitcast(I32)
        anchor = small[:, 80:88].rearrange("p (h e) -> p h e", h=HG)
        mv = small[:, 88:96].rearrange("p (h e) -> p h e", h=HG)
        sd = small[:, 96:100]
        slope = small[:, 100:104]
        act_sum = small[:, 104:106]
        tmp = small[:, 108:128].rearrange("p (k h) -> p k h", h=HG)
        mx = small[:, 128:136].rearrange("p (s h) -> p s h", s=2)
        nb = small[:, 136:144].rearrange("p (s h) -> p s h", s=2)
        OH = small[:, 144:176].rearrange("p (h j) -> p h j", h=HG)
        m8 = OH
        PR = small[:, 176:208].rearrange("p (h j) -> p h j", h=HG)
        tnext = small[:, 208:212]
        good = small[:, 212:216]
        st6 = small[:, 216:240].rearrange("p (h e) -> p h e", h=HG)
        z_tab = small[:, 240:248]
        slope_tab = small[:, 248:256]
        ln_st = small[:, 80:92].rearrange("p (a b) -> p a b", a=2)
        ln_mv = small[:, 96:128].rearrange("p (t c) -> p t c", c=2)
        ln_ve = small[:, 128:144]
        ln_sd = small[:, 144:160]
        ln_r = small[:, 160:176]
        ln_t = small[:, 176:192]
        Rsb = small[:, 256:384]
        rinv = small[:, 384:512]

        s0 = dict(const=sem("const"), ones=sem("ones"), apart=sem("apart"))

        dma = dict(xl=[sem(f"xl{t}") for t in range(NT)], wo=[sem(f"wo{k}") for k in range(4)],
                              xo=[sem(f"xo{k}") for k in range(4)], st=[sem(f"st{k}") for k in range(4)],
                              fx=[sem(f"fx{k}") for k in range(4)], fw=[sem(f"fw{k}") for k in range(4)])

        def layer_sems(L):
            s = dict(**{n: sem(f"{L}_{n}") for n in (
                      "tab", "x_norm", "ln_var", "ln_sd", "tr_full", "tr_free", "pj_full", "pj_free", "s_full",
                      "s_free", "e_ready", "p_ready", "nb_ready", "rinv_ready", "pv_full", "pv_free",
                      "handoff", "shuffled", "roped", "o_full", "o_free", "chain", "bo")})
            s["xl"], s["wo"], s["xo"], s["st"] = dma["xl"], dma["wo"], dma["xo"], dma["st"]
            s["xl0"], s["slot0"] = (0, 0) if L == "A" else (BATCH * 16, BATCH * 32)
            if L == "A":
                s.update({n: sem(f"{L}_{n}") for n in ("stats", "sd", "t_new", "counted", "below", "good", "flag")})
            s["w"] = [sem(f"{L}_w{m}") for m in range(3)]
            s["w_free"] = [sem(f"{L}_wfree{m}") for m in range(3)]
            return s

        def layer(L, topk, src, dst, rope):
            pre = "L0_attn_a_" if L == "A" else "L0_attn_b_"
            return dict(
                s=layer_sems(L), topk=topk, src=src, dst=dst, rope=rope, bias=(L == "B"), gqa=(L == "A"),
                Wq=I[pre + "Wq"], Wk=I[pre + "Wk"], Wv=I[pre + "Wv"], Wo=I[pre + "Wo"],
                b=[I[pre + n] for n in ("bq", "bk", "bv")] if L == "B" else None,
                cos=rope_cos[0 if L == "A" else 1], sin=rope_sin[0 if L == "A" else 1])

        x_in = I["L0_attn_a_hidden_states"].rearrange("b s d -> (b s) d")
        out2 = out.rearrange("b s d -> (b s) d")
        A = layer("A", True, x_in, x1, "half")
        B = layer("B", False, x2, x3, "pairs")

        PIECES = [(kind, m, k) for m in range(3) for kind in ("wt", "mm") for k in range(2)] + [("vt", 2, 0), ("vt", 2, 1)]
        assert len(PIECES) == PJ_GROUP

        def apart(eng):
            eng.sem_inc(s0["apart"], 1)

        def att_sync(sp, L):
            s = L["s"]
            sp.dma_start(COS, L["cos"]).then_inc(s["tab"], 16)
            sp.dma_start(SIN, L["sin"]).then_inc(s["tab"], 16)
            if L["topk"]:
                sp.dma_start(small[:, 240:256], search_d).then_inc(s["tab"], 16)

            def weights(p, g):
                for m, w in enumerate((L["Wq"], L["Wk"], L["Wv"])):
                    sp.wait_ge(s["w_free"][m], p + 1)
                    apart(sp)
                    if L["gqa"] and m:
                        for c in range(HG):
                            sp.dma_start(W_stage[HD * c:HD * c + HD, m, :],
                                         w[bass.ds(g * HD, HD), :]).then_inc(s["w"][m], 16)
                    else:
                        sp.dma_start(W_stage[:, m, :], w[bass.ds(g * P, P), :]).then_inc(s["w"][m], 16)
                    if L["bias"]:
                        bias = L["b"][m].rearrange("(n o) -> n o", o=1)
                        sp.dma_start(bias_st[:, m:m + 1], bias[bass.ds(g * P, P), :]).then_inc(s["w"][m], 16)

            with sp.Fori(0, BATCH) as b:
                for t in range(NT):
                    sp.dma_start(XL[:, t, :], L["src"][bass.ds(b * SEQ + t * P, P), :]).then_inc(s["xl"][t], 16)
                with sp.Fori(0, NG) as g:
                    weights(b * NG + g, g)
                if L["bias"]:
                    sp.wait_ge(s["w_free"][0], (b + 1) * NG + 1)
                    apart(sp)
                    sp.dma_start(bo_row, I["L0_attn_b_bo"].rearrange("(a n) -> a n", a=1)).then_inc(s["bo"], 16)
                sp.wait_ge(s["rinv_ready"], (b + 1) * (NG * NT))
                apart(sp)
                for ro in range(KT):
                    if ro >= 4:
                        sp.wait_ge(s["tr_full"], b * TR_BATCH + (TR_LN + NG * TR_GROUP + 2 * (ro - 3)))
                        apart(sp)
                    sp.dma_start(SEL[:, ro % 4, :], L["Wo"][ro * P:ro * P + P, :]).then_inc(s["wo"][ro % 4], 16)
                sp.wait_ge(s["pv_full"], (b + 1) * (NG * NT))
                apart(sp)
                for t in range(NT + 4):
                    if t >= 4:
                        sp.wait_ge(s["o_free"], b * NT + (t - 4) + 1 + 2)
                        apart(sp)
                        sp.dma_start(L["dst"][bass.ds(b * SEQ + (t - 4) * P, P), :],
                                     EX[:, t % 4, :]).then_inc(s["st"][t % 4], 16)
                    if t < NT:
                        if t >= 4:
                            sp.wait_ge(s["st"][t % 4], b * 32 + (s["slot0"] + 16))
                            apart(sp)
                        sp.dma_start(EX[:, t % 4, :], L["src"][bass.ds(b * SEQ + t * P, P), :]).then_inc(s["xo"][t % 4], 16)
                for k in range(4):
                    sp.wait_ge(s["st"][k], b * 32 + (s["slot0"] + 32))
                    apart(sp)

        def att_tensor(pe, L):
            s = L["s"]
            tr, pj = Tally(s["tr_full"]), Tally(s["pj_full"])

            def tr_slot():
                pe.wait_ge(s["tr_free"], tr.base + (tr.n + 1))
                return TR_ring[:, tr.n % 2, :]

            def piece(p, kind, m, k):
                pe.wait_ge(s["pj_free"], pj.base + (pj.n + 1))
                if kind == "wt":
                    if k == 0:
                        pe.wait_ge(s["w"][m], (p + 1) * (16 * ((HG if L["gqa"] and m else 1) + (1 if L["bias"] else 0))))
                    for c in range(4):
                        ins = pe.transpose(PJ[:, c * P:c * P + P], W_stage[:, m, (4 * k + c) * P:(4 * k + c + 1) * P],
                                           ident[:, :])
                        if m and k == 0 and c == 0:
                            ins.then_inc(s["w_free"][m - 1], 1)
                    pj.mark(ins)
                elif kind == "mm":
                    for kt in range(KT):
                        ins = pe.matmul(PJ[:, :], WT[:, kt, :], XT[:, kt, k * 512:k * 512 + 512],
                                        start=(kt == 0), stop=(kt == KT - 1))
                    pj.mark(ins)
                else:
                    for c in range(4):
                        t = 4 * k + c
                        ins = pe.transpose(PJ[:, c * P:c * P + P], NXT[:, 2, t * P:t * P + P], ident[:, :])
                        if t == 0:
                            ins.then_inc(s["w_free"][2], 1)
                    pj.mark(ins)

            def scores(it, i, heads=range(HG)):
                n = (i + 1) * P
                for h in heads:
                    x = i * HG + h
                    pe.wait_ge(s["s_free"], it * (NT * HG) + (x + 1))
                    q = CUR_QK[HD * h:HD * h + HD, 0, i * P:i * P + P]
                    for c in range(0, n, 512):
                        w = min(512, n - c)
                        last = c + w == n
                        pe.matmul(S_ring[:, x % 2, c:c + w], q, CUR_QK[HD * h:HD * h + HD, 1, c:c + w],
                                  start=True, stop=not last)
                    pe.matmul(S_ring[:, x % 2, n - P:n], ident16[:, :], future16[:, :],
                              start=False, stop=True).then_inc(s["s_full"], 1)

            def attention(it, g, project):
                pe.wait_ge(s["handoff"], it * 3 + 3)
                scores(it, 0)
                for i in range(NT):
                    searched = L["topk"] and i > 0
                    if i + 1 < NT and not searched:
                        scores(it, i + 1)
                    if project:
                        for j in UNIT_PIECES[i]:
                            piece(it + 1, *PIECES[j])
                    if searched:
                        if i + 1 < NT:
                            scores(it, i + 1, (0, 1))
                        pe.wait_ge(s["good"], it * (NT - 1) + i)
                        pe.matmul(PV[0:1, 504:504 + HG], ones[:, 0:1], good, start=True, stop=True).then_inc(s["flag"], 1)
                        if i + 1 < NT:
                            scores(it, i + 1, (2, 3))
                    for h in range(HG):
                        if L["topk"] and i:
                            pe.wait_ge(s["p_ready"], it * (HG * (NT - 1)) + ((i - 1) * HG + h + 1))
                        else:
                            pe.wait_ge(s["e_ready"], it * (HG * NT) + (i * HG + h + 1))
                        for c in range(0, i + 1, 4):
                            slot = tr_slot()
                            for kt in range(c, min(c + 4, i + 1)):
                                ins = pe.transpose(slot[:, (kt - c) * P:(kt - c + 1) * P],
                                                   EX[:, h, kt * P:kt * P + P], ident[:, :])
                            tr.mark(ins)
                    pe.wait_ge(s["tr_free"], tr.base + (tr.n + 2))
                    pe.wait_ge(s["pv_free"], it * NT + (i + 1))
                    for h in range(HG):
                        for kt in range(i + 1):
                            ins = pe.matmul(PV[HD * h:HD * h + HD, 0:P], CUR_V[:, kt, HD * h:HD * h + HD],
                                            PT[:, h * NT + kt, :], start=(kt == 0), stop=(kt == i))
                    ins.then_inc(s["pv_full"], 1)
                    slot = tr_slot()
                    pe.wait_ge(s["rinv_ready"], it * NT + (i + 1))
                    tr.mark(pe.matmul(slot[:, 0:P], rinv, ident[:, :],
                                        start=True, stop=True))

            with pe.Fori(0, BATCH) as b:
                tr.at(b * TR_BATCH)
                pj.at(b * (PJ_GROUP * NG))
                for t in range(NT):
                    pe.wait_ge(s["x_norm"], b * NT + (t + 1))
                    for k in range(2):
                        slot = tr_slot()
                        for c in range(4):
                            ins = pe.transpose(slot[:, c * P:c * P + P], XL[:, t, (4 * k + c) * P:(4 * k + c + 1) * P],
                                               ident[:, :])
                        tr.mark(ins)
                pe.wait_ge(s["tr_free"], tr.base + (tr.n + 2))
                pe.wait_ge(s["o_free"], b * NT + 2)
                for q in PIECES:
                    piece(b * NG, *q)
                with pe.Fori(0, NG - 1) as g:
                    tr.at(b * TR_BATCH + TR_LN + g * TR_GROUP)
                    pj.at(b * (PJ_GROUP * NG) + PJ_GROUP + g * PJ_GROUP)
                    attention(b * NG + g, g, True)
                    assert tr.n == TR_GROUP and pj.n == PJ_GROUP
                tr.at(b * TR_BATCH + TR_LN + (NG - 1) * TR_GROUP)
                attention(b * NG + NG - 1, NG - 1, False)
                WoT = S_sb.rearrange("p a h n -> p (a h) n")
                for ro in range(KT):
                    pe.wait_ge(s["wo"][ro % 4], b * 32 + (s["slot0"] + 16 + 16 * (ro // 4)))
                    for k in range(2):
                        slot = tr_slot()
                        for c in range(4):
                            ins = pe.transpose(slot[:, c * P:c * P + P], SEL[:, ro % 4, (4 * k + c) * P:(4 * k + c + 1) * P],
                                               ident[:, :])
                        tr.mark(ins)
                pe.wait_ge(s["tr_free"], tr.base + (tr.n + 2))
                pe.wait_ge(s["s_free"], (b + 1) * (NG * NT * HG) + 2)
                pe.wait_ge(s["pv_free"], (b + 1) * (NG * NT) + 1)
                if L["bias"]:
                    pe.wait_ge(s["bo"], b * 16 + 16)
                for t in range(NT):
                    pe.wait_ge(s["o_free"], b * NT + (t + 1))
                    for c in range(2):
                        for kt in range(KT):
                            ins = pe.matmul(S_ring[:, t % 2, c * 512:c * 512 + 512], OT[:, kt, t * P:t * P + P],
                                            WoT[:, kt, c * 512:c * 512 + 512], start=(kt == 0),
                                            stop=(kt == KT - 1 and not L["bias"]))
                        if L["bias"]:
                            ins = pe.matmul(S_ring[:, t % 2, c * 512:c * 512 + 512], ones[0:1, :],
                                            bo_row[0:1, c * 512:c * 512 + 512], start=False, stop=True)
                    ins.then_inc(s["o_full"], 1)

        def att_scalar(act, L):
            s = L["s"]
            tr, pj = Tally(s["tr_free"]), Tally(s["pj_free"])
            act.sem_inc(s["tr_free"], 2)
            act.sem_inc(s["pj_free"], 1)

            def tr_out(dst, cols=512, split=4):
                act.wait_ge(s["tr_full"], tr.base + (tr.n + 1))
                src = TR_ring[:, tr.n % 2, 0:cols]
                if split:
                    src = src.rearrange("p (c n) -> p c n", n=P)
                tr.mark(act.copy(dst, src))

            def piece(kind, m, k):
                act.wait_ge(s["pj_full"], pj.base + (pj.n + 1))
                if kind == "wt":
                    pj.mark(act.copy(WT[:, 4 * k:4 * k + 4, :], PJ[:, :].rearrange("p (c n) -> p c n", n=P)))
                elif kind == "mm":
                    dst = NXT[:, m, k * 512:k * 512 + 512]
                    if L["bias"]:
                        pj.mark(act.activation(dst, PJ[:, :], ACT.Identity, bias=bias_st[:, m:m + 1]))
                    else:
                        pj.mark(act.copy(dst, PJ[:, :]))
                else:
                    pj.mark(act.copy(NXV[:, 4 * k:4 * k + 4, :], PJ[:, :].rearrange("p (c n) -> p c n", n=P)))

            def exps(it, i):
                n = (i + 1) * P
                act.wait_ge(s["nb_ready"], it * NT + (i + 1))
                act.wait_ge(s["s_free"], it * (NT * HG) + (i * HG + HG + 2))
                for h in range(HG):
                    if L["topk"] and i:
                        ins = act.activation(EX[:, h, 0:n], S_sb[:, i % 2, h, 0:n], ACT.Exp,
                                             bias=nb[:, i % 2, h:h + 1], scale=EXP_SCALE)
                    else:
                        ins = act.activation(EX[:, h, 0:n], S_sb[:, i % 2, h, 0:n], ACT.Exp,
                                             bias=nb[:, i % 2, h:h + 1], scale=EXP_SCALE,
                                             accum_out=sums[:, i % 2, h:h + 1])
                    ins.then_inc(s["e_ready"], 1)

            def probs_out(i, heads):
                for h in heads:
                    for c in range(0, i + 1, 4):
                        w = min(4, i + 1 - c)
                        tr_out(PT[:, h * NT + c:h * NT + c + w, :], cols=w * P)

            def count(it, i, k):
                n = (i + 1) * P
                act.wait_ge(s["t_new"], it * ((NT - 1) * NC) + ((i - 1) * NC + k + 1))
                for h in ACT_HEADS:
                    act.activation(SEL[:, h, 0:n], S_sb[:, i % 2, h, 0:n], ACT.Sign, bias=points[:, k % 3, h, 1:2],
                                   scale=-1.0, accum_out=act_sum[:, h - 2:h - 1]).then_inc(s["counted"], 1)

            def attention(it, project):
                for i in range(NT):
                    n = (i + 1) * P
                    pieces = [PIECES[j] for j in UNIT_PIECES[i]] if project else []
                    if L["topk"] and i:
                        count(it, i, 0)
                        probs_out(i - 1, (0, 1))
                        count(it, i, 1)
                        probs_out(i - 1, (2, 3))
                        count(it, i, 2)
                        count(it, i, 3)
                        tr_out(Rsb, cols=P, split=0)
                        count(it, i, 4)
                        for q in pieces[:-1]:
                            piece(*q)
                        act.wait_ge(s["below"], it * ((NT - 1) * 2) + i * 2)
                        for h in ACT_HEADS:
                            act.activation(EX[:, h, 0:n], SEL[:, h, 0:n], ACT.Sign, bias=half,
                                           accum_out=act_sum[:, h - 2:h - 1]).then_inc(s["counted"], 1)
                        act.wait_ge(s["counted"], it * ((NT - 1) * 2 * (NC + 1)) + i * 2 * (NC + 1))
                        exps(it, i)
                        for q in pieces[-1:]:
                            piece(*q)
                    else:
                        if i:
                            probs_out(i - 1, range(HG))
                            tr_out(Rsb, cols=P, split=0)
                        exps(it, i)
                        for q in pieces:
                            piece(*q)
                probs_out(NT - 1, range(HG))
                tr_out(Rsb, cols=P, split=0)

            with act.Fori(0, BATCH) as b:
                tr.at(b * TR_BATCH)
                pj.at(b * (PJ_GROUP * NG))
                act.wait_ge(s["ln_var"], b + 1)
                act.activation(ln_sd[:, 0:NT], ln_ve[:, 0:NT], ACT.Sqrt).then_inc(s["ln_sd"], 1)
                for t in range(NT):
                    for k in range(2):
                        tr_out(XT[:, 4 * k:4 * k + 4, t * P:t * P + P])
                for q in PIECES:
                    piece(*q)
                with act.Fori(0, NG - 1) as g:
                    tr.at(b * TR_BATCH + TR_LN + g * TR_GROUP)
                    pj.at(b * (PJ_GROUP * NG) + PJ_GROUP + g * PJ_GROUP)
                    attention(b * NG + g, True)
                tr.at(b * TR_BATCH + TR_LN + (NG - 1) * TR_GROUP)
                attention(b * NG + NG - 1, False)
                WoT = S_sb.rearrange("p a h n -> p (a h) n")
                for ro in range(KT):
                    for k in range(2):
                        tr_out(WoT[:, 4 * k:4 * k + 4, ro * P:ro * P + P])
                assert tr.n == TR_GROUP + TR_WO

        def layer_norm(dve, s, chain, n_tiles, b1, load_wait, tile, eps_to_act, write):
            for t in range(n_tiles):
                load_wait(t)
                x = tile(t)
                if t:
                    chain.reached(dve)
                chain.mark(dve.bn_stats(ln_st[:, 0, :], x[:, 0:512]))
                chain.mark(dve.bn_stats(ln_st[:, 1, :], x[:, 512:1024]))
                chain.reached(dve)
                apart(dve)
                chain.mark(dve.bn_aggr(ln_mv[:, t, :], ln_st))
            chain.reached(dve)
            dve.tensor_scalar(ln_ve[:, 0:n_tiles], ln_mv[:, 0:n_tiles, 1], LN_EPS, None, ALU.add).then_inc(s["ln_var"], 1)
            dve.wait_ge(s["ln_sd"], b1)
            r, tt, ve = ln_r[:, 0:n_tiles], ln_t[:, 0:n_tiles], ln_ve[:, 0:n_tiles]
            chain.mark(dve.reciprocal(r, ln_sd[:, 0:n_tiles]))
            chain.reached(dve)
            chain.mark(dve.tensor_tensor(tt, ve, r, ALU.mult))
            chain.reached(dve)
            chain.mark(dve.tensor_tensor(tt, tt, r, ALU.mult))
            chain.reached(dve)
            chain.mark(dve.tensor_scalar(tt, tt, -0.5, 1.5, ALU.mult, ALU.add))
            chain.reached(dve)
            chain.mark(dve.tensor_tensor(r, r, tt, ALU.mult))
            chain.reached(dve)
            if write is not None:
                for t in range(n_tiles):
                    write(t)

        CH_LN = 3 * NT + 5
        CH_UNIT = 80

        def att_vector(dve, L):
            s = L["s"]
            ch = Tally(s["chain"])
            per_group = {True: (NT - 1) * CH_UNIT, False: 0}[L["topk"]]
            per_batch = CH_LN + NG * per_group
            dve.sem_inc(s["pv_free"], 1)
            dve.sem_inc(s["s_free"], 2)
            dve.sem_inc(s["o_free"], 2)
            for m in range(3):
                dve.sem_inc(s["w_free"][m], 1)

            def finalize(it, g, i):
                dve.wait_ge(s["pv_full"], it * NT + (i + 1))
                dve.wait_ge(s["tr_free"], ch_tr[0] + (sum(TR_UNIT[:i + 1]) + 2))
                dve.tensor_tensor(OT[:, g, i * P:i * P + P], PV[:, 0:P], Rsb, ALU.mult).then_inc(s["pv_free"], 1)

            def shuffle(p1, m):
                dve.wait_ge(s["pj_free"], p1 * PJ_GROUP + (4 * m + 4 + 1))
                apart(dve)
                dve.stream_shuffle(SH[:, m, :], NXT[:, m, :], QK_ROPE[L["rope"]]).then_inc(s["shuffled"], 1)

            ch_tr = [0]

            def step(ins):
                ch.mark(ins)
                ch.reached(dve)

            def scores_out(it, i):
                n = (i + 1) * P
                for h in range(HG):
                    x = i * HG + h
                    dve.wait_ge(s["s_full"], it * (NT * HG) + (x + 1))
                    dve.tensor_scalar(S_sb[:, i % 2, h, 0:n], S_ring[:, x % 2, 0:n], 1.0, -1.0, ALU.mult, ALU.max,
                                      accum_out=mx[:, i % 2, h:h + 1]).then_inc(s["s_free"], 1)
                dve.wait_ge(s["s_free"], it * (NT * HG) + (i * HG + HG + 2))
                dve.tensor_scalar(nb[:, i % 2, :], mx[:, i % 2, :], -EXP_SCALE, None, ALU.mult).then_inc(s["nb_ready"], 1)

            def statistics(it, i):
                every = max(1, i // 2)
                for h in range(HG):
                    ch.mark(dve.bn_stats(st6[:, h, :], S_sb[:, i % 2, h, 0:i * P:every]))
                ch.reached(dve)
                apart(dve)
                for h in range(HG):
                    ins = dve.bn_aggr(mv[:, h, :], st6[:, h, :])
                    if h + 1 < HG:
                        ch.mark(ins)
                    else:
                        ins.then_inc(s["stats"], 1)

            def first_threshold(it, i):
                dve.wait_ge(s["sd"], it * (NT - 1) + i)
                ch.mark(dve.tensor_scalar(slope, sd, slope_tab[:, i:i + 1], None, ALU.mult))
                dve.scalar_tensor_tensor(out=points[:, 0, :, 1], in0=sd, scalar=z_tab[:, i:i + 1], in1=mv[:, :, 0],
                                         op0=ALU.mult, op1=ALU.add).then_inc(s["t_new"], 1)

            def search_step(it, i, k):
                n = (i + 1) * P
                N, Q = points[:, k % 3], points[:, (k - 1) % 3]
                t_next = points[:, (k + 1) % 3, :, 1]
                e, t = N[:, :, 0], N[:, :, 1]
                dve.wait_ge(s["t_new"], it * ((NT - 1) * NC) + ((i - 1) * NC + k + 1))
                for h in range(HG):
                    if h not in ACT_HEADS:
                        ch.mark(dve.tensor_scalar(SEL[:, h, 0:n], S_sb[:, i % 2, h, 0:n], N[:, h, 1:2], -AIM,
                                                  ALU.is_ge, ALU.add, accum_out=N[:, h, 0:1]))
                signs_to_counts(it, i, k, N[:, 2:4, 0])
                if k == 0:
                    step(dve.tensor_scalar(tmp[:, 0, :], e, 0.0, 2 * STEP_OVER, ALU.is_ge, ALU.mult))
                    step(dve.tensor_scalar(tmp[:, 0, :], tmp[:, 0, :], -STEP_OVER, None, ALU.add))
                    step(dve.tensor_tensor(tmp[:, 0, :], tmp[:, 0, :], e, ALU.add))
                    step(dve.tensor_tensor(tmp[:, 0, :], tmp[:, 0, :], slope, ALU.mult))
                    dve.tensor_tensor(t_next, t, tmp[:, 0, :], ALU.add).then_inc(s["t_new"], 1)
                    ch.mark(dve.tensor_copy(anchor, N))
                    ch.mark(dve.tensor_copy(G[:, :, 0:2], N))
                else:
                    if k >= 2 and k + 1 < NC:
                        step(dve.tensor_tensor(tmp[:, 0, :], e, Q[:, :, 0], ALU.mult))
                        step(dve.tensor_scalar(tmp[:, 1, :], tmp[:, 0, :], 0.0, None, ALU.is_lt))
                        apart(dve)
                        step(dve.copy_predicated(anchor, tmp[:, 1, :].bitcast(I32).unsqueeze(2).to_broadcast([P, HG, 2]), Q))
                    if k + 1 < NC:
                        ch.mark(dve.tensor_tensor(tmp[:, 1, :], anchor[:, :, 0], e, ALU.subtract))
                        step(dve.tensor_tensor(tmp[:, 0, :], anchor[:, :, 1], t, ALU.subtract))
                        step(dve.tensor_scalar(tmp[:, 1, :], tmp[:, 1, :], 0.1, None, ALU.add))
                        ch.mark(dve.reciprocal(tmp[:, 2, :], tmp[:, 1, :]))
                        step(dve.tensor_tensor(tmp[:, 0, :], tmp[:, 0, :], e, ALU.mult))
                        step(dve.tensor_tensor(tmp[:, 0, :], tmp[:, 0, :], tmp[:, 2, :], ALU.mult))
                        dve.tensor_tensor(t_next, t, tmp[:, 0, :], ALU.subtract).then_inc(s["t_new"], 1)
                    step(dve.tensor_tensor(tmp[:, 3, :], e, e, ALU.mult))
                    step(dve.tensor_scalar(tmp[:, 4, :], tmp[:, 3, :], (TOP - AIM) ** 2 + 0.5, None, ALU.is_le))
                    apart(dve)
                    ch.mark(dve.copy_predicated(G[:, :, 0:2],
                                                tmp[:, 4, :].bitcast(I32).unsqueeze(2).to_broadcast([P, HG, 2]), N))

            def signs_to_counts(it, i, k, out):
                dve.wait_ge(s["counted"], it * ((NT - 1) * 2 * (NC + 1)) + ((i - 1) * 2 * (NC + 1) + 2 * k + 2))
                step(dve.tensor_scalar(out, act_sum, -0.5, (i + 1) * P / 2 - AIM, ALU.mult, ALU.add))

            def settle(it, i):
                n = (i + 1) * P
                ch.reached(dve)
                for h in (2, 3, 0, 1):
                    ins = dve.scalar_tensor_tensor(out=SEL[:, h, 0:n], in0=S_sb[:, i % 2, h, 0:n], scalar=G[:, h, 1:2],
                                                   in1=S_sb[:, i % 2, h, 0:n], op0=ALU.is_ge, op1=ALU.subtract, reverse1=True)
                    if h in ACT_HEADS:
                        ins.then_inc(s["below"], 1)
                    else:
                        ch.mark(ins)
                dve.wait_ge(s["below"], it * ((NT - 1) * 2) + i * 2)
                ch.reached(dve)
                apart(dve)
                for h in (2, 3, 0, 1):
                    ch.mark(dve.max(G[:, h, 2:10], SEL[:, h, 0:n]))
                signs_to_counts(it, i, NC, G[:, 2:4, 0])
                step(dve.tensor_scalar(tmp[:, 0, :], G[:, :, 0], -1.0, TOP - AIM, ALU.mult, ALU.add))
                step(dve.tensor_tensor(OH, tmp[:, 0, :].unsqueeze(2).to_broadcast([P, HG, 8]),
                                       iota[:, :].unsqueeze(1).to_broadcast([P, HG, 8]), ALU.is_equal))
                for dst, at in ((tstar, 1), (tnext, 2)):
                    step(dve.tensor_tensor(PR, OH, G[:, :, at:at + 8], ALU.mult))
                    step(dve.tensor_reduce(dst, PR, mybir.AxisListType.X, ALU.add))
                dve.tensor_tensor(good, tstar, tnext, ALU.is_gt).then_inc(s["good"], 1)

            def repair(it, i):
                n = (i + 1) * P
                dve.wait_ge(s["flag"], it * (NT - 1) + i)
                step(dve.tensor_reduce(small[0:1, 106:107], PV[0:1, 504:504 + HG], mybir.AxisListType.X, ALU.add))
                step(dve.tensor_copy(ended_well[0:1, :], small[0:1, 106:107]))
                apart(dve)
                rows = dve.value_load(ended_well[0:1, :])
                with dve.If(rows != HG * P):
                    for h in range(HG):
                        dve.max(m8[:, h, :], S_sb[:, i % 2, h, 0:n])
                        dve.drain()
                        dve.match_replace(SEL[:, h, 0:n], m8[:, h, :], S_sb[:, i % 2, h, 0:n], TAKEN)
                        dve.drain()
                        with dve.Fori(0, TOP // 8 - 1):
                            dve.max(m8[:, h, :], SEL[:, h, 0:n])
                            dve.drain()
                            dve.match_replace(SEL[:, h, 0:n], m8[:, h, :], SEL[:, h, 0:n], TAKEN)
                            dve.drain()
                        dve.tensor_scalar(S_sb[:, i % 2, h, 0:n], SEL[:, h, 0:n], TAKEN / 2, None, ALU.is_le)
                    dve.memset(tstar, 0.5)
                    dve.drain()

            def attention(it, b, g, project):
                ch_tr[0] = b * TR_BATCH + TR_LN + g * TR_GROUP
                dve.wait_ge(s["roped"], it * 2 + 2)
                dve.wait_ge(s["pj_free"], it * PJ_GROUP + (PJ_GROUP + 1))
                for m in range(2):
                    dve.tensor_tensor(CUR_QK[:, m, :], NXT[:, m, :], SH[:, m, :], ALU.add).then_inc(s["handoff"], 1)
                dve.tensor_copy(CUR_V, NXV).then_inc(s["handoff"], 1)
                scores_out(it, 0)
                for i in range(NT):
                    n = (i + 1) * P
                    searched = L["topk"] and i > 0
                    if searched:
                        for k in range(NC):
                            search_step(it, i, k)
                        finalize(it, g, i - 1)
                        if project and i in (2, 4):
                            shuffle(it + 1, i // 2 - 1)
                        settle(it, i)
                    if i + 1 < NT:
                        scores_out(it, i + 1)
                        if L["topk"]:
                            statistics(it, i + 1)
                    if i and not searched:
                        finalize(it, g, i - 1)
                        if project and i in (2, 4):
                            shuffle(it + 1, i // 2 - 1)
                    dve.wait_ge(s["e_ready"], it * (HG * NT) + (i * HG + HG))
                    if searched:
                        apart(dve)
                        repair(it, i)
                    if L["topk"] and i + 1 < NT:
                        first_threshold(it, i + 1)
                    if searched:
                        for h in range(HG):
                            dve.scalar_tensor_tensor(out=EX[:, h, 0:n], in0=S_sb[:, i % 2, h, 0:n], scalar=tstar[:, h:h + 1],
                                                     in1=EX[:, h, 0:n], op0=ALU.is_ge, op1=ALU.mult,
                                                     accum_out=sums[:, i % 2, h:h + 1]).then_inc(s["p_ready"], 1)
                        dve.wait_ge(s["p_ready"], it * (HG * (NT - 1)) + i * HG)
                    dve.reciprocal(rinv.rearrange("p (h d) -> p h d", h=HG),
                                   sums[:, i % 2, :].unsqueeze(2).to_broadcast([P, HG, HD])).then_inc(s["rinv_ready"], 1)
                finalize(it, g, NT - 1)

            with dve.Fori(0, BATCH) as b:
                ch.at(b * per_batch)

                def norm(t):
                    dve.tensor_scalar(XL[:, t, :], XL[:, t, :], ln_mv[:, t, 0:1], ln_r[:, t:t + 1], ALU.subtract,
                                      ALU.mult).then_inc(s["x_norm"], 1)

                layer_norm(dve, s, ch, NT, b + 1, lambda t: dve.wait_ge(s["xl"][t], b * 16 + (s["xl0"] + 16)), lambda t: XL[:, t, :],
                           None, norm)
                assert ch.n == CH_LN, ch.n
                for m in range(2):
                    shuffle(b * NG, m)
                with dve.Fori(0, NG - 1) as g:
                    ch.at(b * per_batch + CH_LN + g * per_group)
                    attention(b * NG + g, b, g, True)
                    assert ch.n == per_group, (ch.n, per_group)
                ch.at(b * per_batch + CH_LN + (NG - 1) * per_group)
                attention(b * NG + NG - 1, b, NG - 1, False)
                for t in range(NT):
                    dve.wait_ge(s["o_full"], b * NT + (t + 1))
                    dve.wait_ge(s["xo"][t % 4], b * 32 + (s["slot0"] + 16 + 16 * (t // 4)))
                    dve.tensor_tensor(EX[:, t % 4, :], EX[:, t % 4, :], S_ring[:, t % 2, :],
                                      ALU.add).then_inc(s["o_free"], 1)

        def att_pool(pool, L):
            s = L["s"]

            def rope(p1, m):
                pool.wait_ge(s["shuffled"], p1 * 2 + (m + 1))
                pool.tensor_tensor(SH[:, m, :], SH[:, m, :], SIN, ALU.mult)
                pool.tensor_tensor(NXT[:, m, :], NXT[:, m, :], COS, ALU.mult).then_inc(s["roped"], 1)

            def attention(it, project):
                for i in range(1, NT):
                    if project and i in (3, 5):
                        rope(it + 1, i // 2 - 1)
                    if L["topk"]:
                        pool.wait_ge(s["stats"], it * (NT - 1) + i)
                        pool.tensor_tensor(sd, mv[:, :, 1], one_half, ALU.pow).then_inc(s["sd"], 1)

            pool.wait_ge(s["tab"], 48 if L["topk"] else 32)
            with pool.Fori(0, BATCH) as b:
                for m in range(2):
                    rope(b * NG, m)
                with pool.Fori(0, NG - 1) as g:
                    attention(b * NG + g, True)
                attention(b * NG + NG - 1, False)

        take = carve()
        FX = take(NTOK, DM)
        NCOL = DM + HID + E * R
        FW = take(KT, NCOL)
        F_stage = take(4, DM)
        F_gw1 = take(DM)
        F_B = take(DM)
        F_xn = take(2, DM)
        F_xT = take(2, KT, P)
        F_tmp = take(NTOK, P)
        F_h = take(NTOK, HID)
        F_h2 = take(NTOK, HID)
        F_hT = take(NTOK, P)
        F_tT = F_hT
        F_g = take(NTOK, E)
        F_top = take(NTOK, E)
        F_idx = take(NTOK, E)
        F_oh = take(NTOK, 2, E)
        F_w = take(NTOK, E)
        F_w2 = take(NTOK, E)
        F_cnt = take(2 * E)
        F_p = take(NTOK, 4)
        F_mu = take(NTOK)
        F_va = take(NTOK)
        F_vb = take(NTOK)
        F_row = take(4, HID)
        F_gw2T = take(E)
        fsmall = take(512)
        f_st = fsmall[:, 0:12].rearrange("p (a b) -> p a b", a=2)
        f_mv = fsmall[:, 16:48].rearrange("p (t c) -> p t c", c=2)
        f_ve, f_sd, f_r, f_t = (fsmall[:, 64 + 16 * k:80 + 16 * k] for k in range(4))

        def ffn_layer(n, src, dst):
            s = dict(**{q: sem(f"F{n}_{q}") for q in (
                      "ln_var", "ln_sd", "x_norm", "tr_full", "tr_free", "m_full", "m_free", "a_full", "a_free", "w2",
                      "h_ln", "h_sd", "chain", "h_ready", "gates", "exp_in", "exp_out", "oh", "cnt", "t_ready", "l_full",
                      "l_done", "st", "loraA", "gw1", "misc", "h_in")})
            s["x"], s["wl"] = dma["fx"], dma["fw"]
            s["x0"], s["wl0"] = (0, 0) if n == 1 else (64, 32)
            return dict(s=s, src=src, dst=dst)

        F1 = ffn_layer(1, x1, x2)
        F2 = ffn_layer(2, x3, out2)
        FPRE = "L0_ffn_"

        def ffn_sync(sp, F):
            s = F["s"]
            for k in range(4):
                for t in range(4 * k, 4 * k + 4):
                    sp.dma_start(FX[:, t, :], F["src"][t * P:t * P + P, :]).then_inc(s["x"][k], 16)
            for ro in range(KT):
                if ro >= 4:
                    sp.wait_ge(s["tr_full"], 2 * (ro - 3))
                sp.dma_start(F_stage[:, ro % 4, :], I[FPRE + "weight"][ro * P:ro * P + P, :]).then_inc(s["wl"][ro % 4], 16)
            sp.dma_start(F_gw1[0:HID, :], I[FPRE + "gw1"]).then_inc(s["gw1"], 16)
            for e in range(E):
                for kt in range(KT):
                    sp.dma_start(FW[:, kt, DM + HID + e * R:DM + HID + e * R + R],
                                 I[FPRE + "lora_A"][e, kt * P:kt * P + P, :]).then_inc(s["loraA"], 16)
            sp.dma_start(F_B, I[FPRE + "lora_B"].rearrange("e r o -> (e r) o")).then_inc(s["misc"], 16)
            for k, nme in enumerate(("gb1", "ln_gamma", "ln_beta", "gb2")):
                w = HID if k < 3 else E
                sp.dma_start(F_row[:, k, 0:w], I[FPRE + nme].partition_broadcast(P)).then_inc(s["misc"], 16)
            sp.dma_start(F_gw2T[0:HID, :], I[FPRE + "gw2"].rearrange("e f -> f e"),
                         allow_slow_non_contiguous=True).then_inc(s["misc"], 16)
            for t in range(NTOK):
                sp.wait_ge(s["l_done"], t + 1)
                sp.dma_start(F["dst"][t * P:t * P + P, :], FX[:, t, :]).then_inc(s["st"], 16)
            sp.wait_ge(s["st"], 16 * NTOK)

        N_MISC = 6
        T_W = 2 * KT + 2

        def ffn_tensor(pe, F):
            s = F["s"]
            tr = Tally(s["tr_full"])

            def tr_slot():
                pe.wait_ge(s["tr_free"], tr.base + (tr.n + 1))
                return TR_ring[:, tr.n % 2, :]

            for ro in range(KT):
                pe.wait_ge(s["wl"][ro % 4], s["wl0"] + 16 * (1 + ro // 4))
                for k in range(2):
                    slot = tr_slot()
                    for c in range(4):
                        ins = pe.transpose(slot[:, c * P:c * P + P],
                                           F_stage[:, ro % 4, (4 * k + c) * P:(4 * k + c + 1) * P], ident[:, :])
                    tr.mark(ins)
            pe.wait_ge(s["gw1"], 16)
            for k in range(2):
                slot = tr_slot()
                for c in range(4):
                    kt = 4 * k + c
                    ins = pe.transpose(slot[:, c * HID:c * HID + HID], F_gw1[0:HID, kt * P:kt * P + P],
                                       ident[0:HID, 0:HID])
                tr.mark(ins)
            pe.wait_ge(s["tr_free"], tr.base + (tr.n + 2))
            pe.wait_ge(s["loraA"], 16 * E * KT)
            with pe.Fori(0, NTOK // 2) as tp:
                tr.at(tp * 4 + T_W)
                for q in range(2):
                    pe.wait_ge(s["x_norm"], tp * 2 + (q + 1))
                    for k in range(2):
                        slot = tr_slot()
                        for c in range(4):
                            ins = pe.transpose(slot[:, c * P:c * P + P], F_xn[:, q, (4 * k + c) * P:(4 * k + c + 1) * P],
                                               ident[:, :])
                        tr.mark(ins)
                    pe.wait_ge(s["tr_free"], tr.base + (tr.n + 2))
                    pe.wait_ge(s["m_free"], tp * 2 + (q + 1))
                    pe.wait_ge(s["a_free"], tp * 2 + (q + 1))
                    aux = (PJ, PV)[q]
                    for kt in range(KT):
                        for c in range(2):
                            ins = pe.matmul(S_ring[:, q, c * 512:c * 512 + 512], F_xT[:, q, kt, :],
                                            FW[:, kt, c * 512:c * 512 + 512], start=(kt == 0), stop=(kt == KT - 1))
                        if kt == KT - 1:
                            ins.then_inc(s["m_full"], 1)
                        ins = pe.matmul(aux[:, 0:HID + E * R], F_xT[:, q, kt, :], FW[:, kt, DM:NCOL],
                                        start=(kt == 0), stop=(kt == KT - 1))
                    ins.then_inc(s["a_full"], 1)
            tr.at(4 * (NTOK // 2) + T_W)
            pe.wait_ge(s["h_ready"], 1)
            for c in range(4):
                slot = tr_slot()
                for t in range(4 * c, 4 * c + 4):
                    ins = pe.transpose(slot[0:HID, (t % 4) * P:(t % 4 + 1) * P], F_h[:, t, :], ident[:, :])
                tr.mark(ins)
            pe.wait_ge(s["tr_free"], tr.base + (tr.n + 2))
            pe.wait_ge(s["misc"], 16 * N_MISC)
            pe.wait_ge(s["a_free"], NTOK + 2)
            for t in range(NTOK):
                ins = pe.matmul(PJ[:, t * E:t * E + E], F_hT[0:HID, t, :], F_gw2T[0:HID, :], start=True, stop=True)
            ins.then_inc(s["gates"], 1)
            pe.wait_ge(s["oh"], 1)
            for t in range(NTOK):
                ins = pe.matmul(PV[:, 0:2 * E], ones[:, :], F_oh[:, t, :, :].rearrange("p k e -> p (k e)"),
                                start=(t == 0), stop=(t == NTOK - 1))
            ins.then_inc(s["cnt"], 1)
            pe.wait_ge(s["t_ready"], 1)
            for c in range(4):
                slot = tr_slot()
                for t in range(4 * c, 4 * c + 4):
                    ins = pe.transpose(slot[:, (t % 4) * P:(t % 4 + 1) * P], F_tmp[:, t, :], ident[:, :])
                tr.mark(ins)
            pe.wait_ge(s["m_free"], NTOK + 2)
            for t in range(NTOK):
                if t % 4 == 0:
                    pe.wait_ge(s["tr_free"], tr.base + (tr.n - 4 + t // 4 + 1 + 2))
                if t >= 2:
                    pe.wait_ge(s["l_done"], t - 1)
                for c in range(2):
                    ins = pe.matmul(S_ring[:, t % 2, c * 512:c * 512 + 512], F_tT[:, t, :],
                                    F_B[:, c * 512:c * 512 + 512], start=True, stop=True)
                ins.then_inc(s["l_full"], 1)

        def ffn_scalar(act, F):
            s = F["s"]
            tr = Tally(s["tr_free"])
            act.sem_inc(s["tr_free"], 2)
            act.sem_inc(s["a_free"], 2)

            def tr_out(dst, cols=512, parts=P, n=P):
                act.wait_ge(s["tr_full"], tr.base + (tr.n + 1))
                tr.mark(act.copy(dst, TR_ring[0:parts, tr.n % 2, 0:cols].rearrange("p (c n) -> p c n", n=n)))

            for ro in range(KT):
                for k in range(2):
                    tr_out(FW[:, 4 * k:4 * k + 4, ro * P:ro * P + P])
            for k in range(2):
                tr_out(FW[:, 4 * k:4 * k + 4, DM:DM + HID], cols=4 * HID, n=HID)
            act.wait_ge(s["ln_var"], 1)
            act.activation(f_sd, f_ve, ACT.Sqrt).then_inc(s["ln_sd"], 1)
            with act.Fori(0, NTOK // 2) as tp:
                tr.at(tp * 4 + T_W)
                for q in range(2):
                    for k in range(2):
                        act.wait_ge(s["tr_full"], tr.base + (tr.n + 1))
                        tr.mark(act.copy(F_xT[:, q, 4 * k:4 * k + 4, :],
                                           TR_ring[:, tr.n % 2, :].rearrange("p (c n) -> p c n", n=P)))
                    aux = (PJ, PV)[q]
                    act.wait_ge(s["a_full"], tp * 2 + (q + 1))
                    act.copy(F_h[:, tp * 2 + q, :], aux[:, 0:HID]).then_inc(s["h_in"], 1)
                    act.copy(F_tmp[:, tp * 2 + q, :], aux[:, HID:HID + E * R]).then_inc(s["a_free"], 1)
            tr.at(4 * (NTOK // 2) + T_W)

            def tr_out2(dst, parts=P):
                act.wait_ge(s["tr_full"], tr.base + (tr.n + 1))
                tr.mark(act.copy(dst, TR_ring[0:parts, tr.n % 2, :].rearrange("p (c n) -> p c n", n=P)))

            act.wait_ge(s["h_ln"], 1)
            act.activation(F_vb, F_va, ACT.Sqrt).then_inc(s["h_sd"], 1)
            for c in range(4):
                tr_out2(F_hT[0:HID, 4 * c:4 * c + 4, :], parts=HID)
            act.wait_ge(s["exp_in"], 1)
            act.activation(F_p[:, :, 1], F_p[:, :, 0], ACT.Exp).then_inc(s["exp_out"], 1)
            for c in range(4):
                tr_out2(F_tT[:, 4 * c:4 * c + 4, :])

        def ffn_vector(dve, F):
            s = F["s"]
            ch = Tally(s["chain"])
            dve.sem_inc(s["m_free"], 2)

            def step(ins):
                ch.mark(ins)
                ch.reached(dve)

            for t in range(NTOK):
                if t % 4 == 0:
                    dve.wait_ge(s["x"][t // 4], s["x0"] + 64)
                if t:
                    ch.reached(dve)
                ch.mark(dve.bn_stats(f_st[:, 0, :], FX[:, t, 0:512]))
                step(dve.bn_stats(f_st[:, 1, :], FX[:, t, 512:1024]))
                ch.mark(dve.bn_aggr(f_mv[:, t, :], f_st))
            ch.reached(dve)
            dve.tensor_scalar(f_ve, f_mv[:, :, 1], LN_EPS, None, ALU.add).then_inc(s["ln_var"], 1)

            def inv_sqrt(r, sd, ve, tt):
                step(dve.reciprocal(r, sd))
                step(dve.tensor_tensor(tt, ve, r, ALU.mult))
                step(dve.tensor_tensor(tt, tt, r, ALU.mult))
                step(dve.tensor_scalar(tt, tt, -0.5, 1.5, ALU.mult, ALU.add))
                step(dve.tensor_tensor(r, r, tt, ALU.mult))

            dve.wait_ge(s["ln_sd"], 1)
            inv_sqrt(f_r, f_sd, f_ve, f_t)

            def norm(t, q):
                dve.tensor_scalar(F_xn[:, q, :], FX[:, t, :], f_mv[:, bass.ds(t, 1), 0], f_r[:, bass.ds(t, 1)],
                                  ALU.subtract, ALU.mult).then_inc(s["x_norm"], 1)

            norm(0, 0)
            norm(1, 1)
            CT = ch.n
            for tp in range(NTOK // 2):
                for q in range(2):
                    t = 2 * tp + q
                    dve.wait_ge(s["m_full"], t + 1)
                    if t + 2 < NTOK:
                        norm(t + 2, q)
                    dve.tensor_tensor(FX[:, t, :], FX[:, t, :], S_ring[:, q, :], ALU.add).then_inc(s["m_free"], 1)

            dve.wait_ge(s["h_in"], NTOK)
            dve.wait_ge(s["misc"], 16 * N_MISC)

            def row(k, w=HID):
                return F_row[:, k, 0:w].unsqueeze(1).to_broadcast([P, NTOK, w])

            def col(a, w):
                return a.unsqueeze(2).to_broadcast([P, NTOK, w])

            step(dve.tensor_tensor(F_h, F_h, row(0), ALU.add))
            step(dve.tensor_reduce(F_mu, F_h, mybir.AxisListType.X, ALU.add))
            step(dve.tensor_scalar(F_mu, F_mu, 1.0 / HID, None, ALU.mult))
            step(dve.tensor_tensor(F_h, F_h, col(F_mu, HID), ALU.subtract))
            step(dve.tensor_tensor(F_h2, F_h, F_h, ALU.mult))
            step(dve.tensor_reduce(F_va, F_h2, mybir.AxisListType.X, ALU.add))
            dve.tensor_scalar(F_va, F_va, 1.0 / HID, LN_EPS, ALU.mult, ALU.add).then_inc(s["h_ln"], 1)
            dve.wait_ge(s["h_sd"], 1)
            inv_sqrt(F_mu, F_vb, F_va, F_p[:, :, 0])
            step(dve.tensor_tensor(F_h, F_h, col(F_mu, HID), ALU.mult))
            step(dve.tensor_tensor(F_h, F_h, row(1), ALU.mult))
            step(dve.tensor_tensor(F_h, F_h, row(2), ALU.add))
            dve.tensor_scalar(F_h, F_h, 0.0, None, ALU.max).then_inc(s["h_ready"], 1)
            dve.wait_ge(s["gates"], 1)
            step(dve.tensor_tensor(F_g, PJ[:, 0:NTOK * E].rearrange("p (t e) -> p t e", e=E), row(3, E), ALU.add))
            for t in range(NTOK):
                ch.mark(dve.max(F_top[:, t, :], F_g[:, t, :]))
            ch.reached(dve)
            for t in range(NTOK):
                ch.mark(dve.max_index(F_idx[:, t, :].bitcast(U32), F_top[:, t, :], F_g[:, t, :]))
            ch.reached(dve)
            step(dve.tensor_copy(F_w2, F_idx.bitcast(U32)))
            for k in range(2):
                ch.mark(dve.tensor_tensor(F_oh[:, :, k, :], iota[:, :].unsqueeze(1).to_broadcast([P, NTOK, E]),
                                            col(F_w2[:, :, k], E), ALU.is_equal))
            ch.reached(dve)
            dve.tensor_tensor(F_p[:, :, 0], F_top[:, :, 1], F_top[:, :, 0], ALU.subtract).then_inc(s["exp_in"], 1)
            dve.drain().then_inc(s["oh"], 1)
            dve.wait_ge(s["exp_out"], 1)
            step(dve.tensor_scalar(F_p[:, :, 2], F_p[:, :, 1], 1.0, None, ALU.add))
            step(dve.reciprocal(F_p[:, :, 3], F_p[:, :, 2]))
            step(dve.tensor_scalar(F_p[:, :, 2], F_p[:, :, 3], 1.0 / R, None, ALU.mult))
            step(dve.tensor_tensor(F_p[:, :, 3], F_p[:, :, 2], F_p[:, :, 1], ALU.mult))
            dve.wait_ge(s["cnt"], 1)
            step(dve.tensor_scalar(F_cnt, PV[:, 0:2 * E], float(CAPACITY), None, ALU.is_le))
            for k, dst in enumerate((F_w, F_w2)):
                allowed = F_cnt[:, k * E:k * E + E].unsqueeze(1).to_broadcast([P, NTOK, E])
                step(dve.tensor_tensor(dst, F_oh[:, :, k, :], allowed, ALU.mult))
                step(dve.tensor_tensor(dst, dst, col(F_p[:, :, 2 + k], E), ALU.mult))
            step(dve.tensor_tensor(F_w, F_w, F_w2, ALU.add))
            tmp = F_tmp.rearrange("p t (e r) -> p (t e) r", r=R)
            w = F_w.rearrange("p t e -> p (t e)").unsqueeze(2).to_broadcast([P, NTOK * E, R])
            dve.wait_ge(s["a_free"], NTOK + 2)
            dve.tensor_tensor(tmp, tmp, w, ALU.mult).then_inc(s["t_ready"], 1)
            for t in range(NTOK):
                dve.wait_ge(s["l_full"], t + 1)
                dve.tensor_tensor(FX[:, t, :], FX[:, t, :], S_ring[:, t % 2, :], ALU.add).then_inc(s["l_done"], 1)

        block = ctx.enter_context(nc.Block())

        @block.sync
        def _(sp):
            sp.dma_start(ident[:, :], ident_d).then_inc(s0["const"], 16)
            sp.dma_start(ones[:, :], future_d).then_inc(s0["const"], 16)
            sp.dma_start(iota[:, :], iota_d).then_inc(s0["const"], 16)
            att_sync(sp, A)
            ffn_sync(sp, F1)
            att_sync(sp, B)
            ffn_sync(sp, F2)

        @block.tensor
        def _(pe):
            pe.wait_ge(s0["const"], 48)
            pe.wait_ge(s0["ones"], 4)
            att_tensor(pe, A)
            ffn_tensor(pe, F1)
            att_tensor(pe, B)
            ffn_tensor(pe, F2)

        @block.scalar
        def _(act):
            act.wait_ge(s0["ones"], 4)
            att_scalar(act, A)
            ffn_scalar(act, F1)
            att_scalar(act, B)
            ffn_scalar(act, F2)

        @block.vector
        def _(dve):
            dve.wait_ge(s0["const"], 48)
            dve.tensor_copy(ident16[:, :], ident[:, :]).then_inc(s0["ones"], 1)
            dve.tensor_copy(future16[:, :], ones[:, :]).then_inc(s0["ones"], 1)
            dve.wait_ge(s0["ones"], 2)
            dve.memset(halves[:, :], 0.5).then_inc(s0["ones"], 1)
            dve.memset(ones[:, :], 1.0).then_inc(s0["ones"], 1)
            dve.wait_ge(A["s"]["tab"], 48)
            att_vector(dve, A)
            ffn_vector(dve, F1)
            att_vector(dve, B)
            ffn_vector(dve, F2)

        @block.gpsimd
        def _(pool):
            pool.wait_ge(s0["ones"], 4)
            att_pool(pool, A)
            att_pool(pool, B)


_INS = ["L0_attn_a_hidden_states", "L0_attn_a_Wq", "L0_attn_a_Wk", "L0_attn_a_Wv", "L0_attn_a_Wo",
        "L0_attn_b_Wq", "L0_attn_b_bq", "L0_attn_b_Wk", "L0_attn_b_bk", "L0_attn_b_Wv", "L0_attn_b_bv",
        "L0_attn_b_Wo", "L0_attn_b_bo", "L0_ffn_weight", "L0_ffn_lora_A", "L0_ffn_lora_B", "L0_ffn_gw1",
        "L0_ffn_gb1", "L0_ffn_ln_gamma", "L0_ffn_ln_beta", "L0_ffn_gw2", "L0_ffn_gb2"]


def tables():
    pos = np.arange(SEQ, dtype=np.float32)
    inv = (1.0 / np.power(np.float32(10000.0), np.arange(0, HD, 2, dtype=np.float32) / np.float32(HD))).astype(np.float32)
    ang = (pos[None, :] * inv[:, None]).astype(np.float32)
    cos, sin = np.cos(ang).astype(np.float32), np.sin(ang).astype(np.float32)
    d = np.arange(HD)
    half, pairs = d % (HD // 2), d // 2
    sign_half = np.where(d < HD // 2, -1.0, 1.0).astype(np.float32)
    sign_pairs = np.where(d % 2 == 0, -1.0, 1.0).astype(np.float32)
    c = np.stack([np.tile(cos[half], (HG, 1)), np.tile(cos[pairs], (HG, 1))])
    s = np.stack([np.tile(sin[half] * sign_half[:, None], (HG, 1)), np.tile(sin[pairs] * sign_pairs[:, None], (HG, 1))])
    k = np.float32(QK_SCALE)
    future = np.where(np.arange(P)[None, :] > np.arange(P)[:, None], FUTURE, 0.0)
    x = np.linspace(-8.0, 8.0, 16001)
    cdf = np.cumsum(np.exp(-x * x / 2))
    keys = np.maximum(np.arange(NT)[None, :] * P + np.arange(P)[:, None] + 1, P + 1)
    z = np.interp(1.0 - AIM / keys, cdf / cdf[-1], x)
    slope = 1.0 / (keys * np.exp(-z * z / 2) / np.sqrt(2 * np.pi))
    return {
        "rope_cos": (c * k).astype(np.float32), "rope_sin": (s * k).astype(np.float32),
        "ident": np.eye(P, dtype=np.float32),
        "future": future.astype(np.float32),
        "expert_ids": np.tile(np.arange(E, dtype=np.float32), (P, 1)),
        "search": np.concatenate([z, slope], axis=1).astype(np.float32),
    }


def kernel(**inputs):
    import numpy as _np
    import concourse.bacc as _bacc
    from concourse import mybir as _mybir
    from concourse.bass_utils import run_bass_kernel_spmd as _run

    nc = _bacc.Bacc("TRN2", target_bir_lowering=False, num_devices=1)
    arrays, named = {}, {}
    for name in _INS:
        a = _np.ascontiguousarray(inputs[name])
        arrays[f"in_{name}"] = a
        named[name] = nc.dram_tensor(f"in_{name}", a.shape, _mybir.dt.from_np(a.dtype), kind="ExternalInput").ap()
    consts = []
    for name, a in tables().items():
        arrays[f"const_{name}"] = a
        consts.append(nc.dram_tensor(f"const_{name}", a.shape, _mybir.dt.from_np(a.dtype), kind="ExternalInput").ap())
    scratch = [nc.dram_tensor(f"x{k}", (BATCH * SEQ, DM), _mybir.dt.float32, kind="Internal").ap() for k in (1, 2, 3)]
    out = nc.dram_tensor("out", (BATCH, SEQ, DM), _mybir.dt.float32, kind="ExternalOutput").ap()
    build(nc, named, *consts, *scratch, out)
    r = _run(nc, [arrays], core_ids=[0])
    return r.results[0]["out"]
```

```python
from contextlib import ExitStack

import numpy as np

import concourse.bass as bass
from concourse import mybir

F32 = mybir.dt.float32
F32R = mybir.dt.float32r
BF16 = mybir.dt.bfloat16
U32 = mybir.dt.uint32
I32 = mybir.dt.int32
ALU = mybir.AluOpType
ACT = mybir.ActivationFunctionType

P = 128
BATCH, SEQ, DM = 2, 1024, 1024
NH, HD = 32, 32
HG = P // HD
NG = NH // HG
NT = SEQ // P
KT = DM // P
NTOK = BATCH * NT
ARENA = 43520
TOP = 128
E, R = 8, 16
HID = 4 * E
CAPACITY = int(3.0 * BATCH * SEQ / E)
LN_EPS = 1e-5

QK_SCALE = 2.0 ** -20
EXP_SCALE = (1.0 / (QK_SCALE * QK_SCALE)) / float(np.sqrt(np.float32(HD)))
FUTURE = -0.25
TAKEN = -1.0

TR_LN = 2 * NT
TR_UNIT = [HG * -(-(i + 1) // 4) + 1 for i in range(NT)]
TR_GROUP = sum(TR_UNIT)
TR_WO = 2 * KT
TR_BATCH = TR_LN + NG * TR_GROUP + TR_WO
PJ_GROUP = 14

NC = 5
CMIN = TOP - 7
AIM = (CMIN + TOP) / 2.0
STEP_OVER = 2.0
ACT_HEADS = (2, 3)
UNIT_PIECES = {True: [(), (0, 1), (2,), (3,), (4, 5, 6), (7, 8, 9), (10, 11), (12, 13)],
               False: [(0, 1, 2), (3, 4, 5), (6,), (7, 8, 9), (10,), (11,), (12, 13), ()]}
ROTATED_AT = {True: (4, 6), False: (2, 4)}
QK_ROPE = {"half": [(d + 16) % 32 for d in range(32)], "pairs": [d ^ 1 for d in range(32)]}


class Tally:

    def __init__(self, sem):
        self.sem, self.base, self.n = sem, 0, 0

    def at(self, base):
        self.base, self.n = base, 0

    def mark(self, ins):
        ins.then_inc(self.sem, 1)
        self.n += 1
        return self.n

    def reached(self, eng, n=None):
        eng.wait_ge(self.sem, self.base + (self.n if n is None else n))


def build(nc, I, rope_cos, rope_sin, ident_d, future_d, iota_d, search_d, x1, x2, x3, out):
    ctx = ExitStack()
    with ctx:
        def sb(name, shape, dt=F32):
            return ctx.enter_context(nc.sbuf_tensor(name, shape, dt))

        def sem(name):
            return ctx.enter_context(nc.semaphore(name))

        ident = sb("ident", [P, P])
        ident16 = sb("ident16", [P, P], BF16)
        future16 = sb("future16", [P, P], BF16)
        ones = sb("ones", [P, P])
        iota = sb("iota", [P, E])
        halves = sb("halves", [P, HG])
        half, one_half = halves[:, 0:1], halves[:, :]
        QS = sb("QS", [P, HG, SEQ], F32R)
        KS_A = sb("KS_A", [P, 1, SEQ], F32R)
        arena = sb("arena", [P, ARENA])
        with nc.sbuf_tensor("SEL", [P, HG, SEQ], F32) as SEL:
            pass
        KS_B = sb("KS_B", [P, HG, SEQ], F32R)

        S_ring = ctx.enter_context(nc.psum_tensor("S_ring", [P, 2, 1024], F32))
        TR_ring = ctx.enter_context(nc.psum_tensor("TR_ring", [P, 2, 512], F32))
        PJ = ctx.enter_context(nc.psum_tensor("PJ", [P, 512], F32))
        PV = ctx.enter_context(nc.psum_tensor("PV", [P, 512], F32))

        def carve():
            at = [0]

            def take(*dims):
                n = int(np.prod(dims))
                a = arena[:, at[0]:at[0] + n]
                at[0] += n
                assert at[0] <= ARENA, at[0]
                if len(dims) == 2:
                    a = a.rearrange("p (a b) -> p a b", a=dims[0])
                if len(dims) == 3:
                    a = a.rearrange("p (a b c) -> p a b c", a=dims[0], b=dims[1])
                return a
            return take

        take = carve()
        XT = take(KT, SEQ)
        OT = take(NG, SEQ)
        XL = OT
        W_stage = take(DM)
        VT = W_stage
        bo_row = W_stage[0:1, :]
        WT = take(KT, P)
        NXT = take(2, SEQ)
        SH = take(2, SEQ)
        NXV = take(NT, P)
        CUR_V = take(NT, P)
        S_sb = take(2, HG, SEQ)
        EX = take(HG, SEQ)
        PT = take(HG * NT, P)
        WO = PT.rearrange("p (s c) n -> p s (c n)", s=4)
        COS = take(SEQ)
        SIN = take(SEQ)
        small = take(512)
        G = small[:, 0:40].rearrange("p (h e) -> p h e", h=HG)
        points = small[:, 40:64].rearrange("p (s h e) -> p s h e", s=3, h=HG)
        tstar = small[:, 64:68]
        sums = small[:, 68:76].rearrange("p (s h) -> p s h", s=2)
        bias_st = small[:, 76:79]
        ended_well = small[:, 79:80].bitcast(I32)
        anchor = small[:, 80:88].rearrange("p (h e) -> p h e", h=HG)
        mv = small[:, 88:96].rearrange("p (h e) -> p h e", h=HG)
        sd = small[:, 96:100]
        slope = small[:, 100:104]
        act_sum = small[:, 104:106]
        tmp = small[:, 108:128].rearrange("p (k h) -> p k h", h=HG)
        mx = small[:, 128:136].rearrange("p (s h) -> p s h", s=2)
        nb = small[:, 136:144].rearrange("p (s h) -> p s h", s=2)
        OH = small[:, 144:176].rearrange("p (h j) -> p h j", h=HG)
        m8 = OH
        PR = small[:, 176:208].rearrange("p (h j) -> p h j", h=HG)
        tnext = small[:, 208:212]
        good = small[:, 212:216]
        st6 = small[:, 216:240].rearrange("p (h e) -> p h e", h=HG)
        z_tab = small[:, 240:248]
        slope_tab = small[:, 248:256]
        ln_st = small[:, 80:92].rearrange("p (a b) -> p a b", a=2)
        ln_mv = small[:, 96:128].rearrange("p (t c) -> p t c", c=2)
        ln_ve = small[:, 128:144]
        ln_sd = small[:, 144:160]
        ln_r = small[:, 160:176]
        ln_t = small[:, 176:192]
        rsum = tmp[:, 4, :]
        Rsb = small[:, 256:384]
        rinv = small[:, 384:512]

        s0 = dict(const=sem("const"), ones=sem("ones"), apart=sem("apart"))

        dma = dict(xl=[sem(f"xl{t}") for t in range(NT)], wo=[sem(f"wo{k}") for k in range(4)],
                              xo=[sem(f"xo{k}") for k in range(4)], st=[sem(f"st{k}") for k in range(4)],
                              fx=[sem(f"fx{k}") for k in range(4)], fw=[sem(f"fw{k}") for k in range(4)])

        def layer_sems(L):
            s = dict(**{n: sem(f"{L}_{n}") for n in (
                      "tab", "x_norm", "ln_var", "ln_sd", "tr_full", "tr_free", "pj_full", "pj_free", "s_full",
                      "s_free", "e_ready", "p_ready", "nb_ready", "rinv_ready", "pv_full", "pv_free",
                      "handoff", "shuffled", "rope_step", "roped", "stacked", "stacked_k", "stacked_low", "o_full", "o_free", "chain", "bo")})
            s["xl"], s["wo"], s["xo"], s["st"] = dma["xl"], dma["wo"], dma["xo"], dma["st"]
            s["xl0"], s["slot0"] = (0, 0) if L == "A" else (BATCH * 16, BATCH * 32)
            if L == "A":
                s.update({n: sem(f"{L}_{n}") for n in ("stats", "sd", "t_new", "counted", "below", "good", "flag")})
            s["w"] = [sem(f"{L}_w{m}") for m in range(3)]
            return s

        def layer(L, topk, src, dst, rope):
            pre = "L0_attn_a_" if L == "A" else "L0_attn_b_"
            return dict(
                s=layer_sems(L), topk=topk, src=src, dst=dst, rope=rope, bias=(L == "B"), gqa=(L == "A"),
                KS=KS_A if L == "A" else KS_B, key_heads=1 if L == "A" else HG,
                Wq=I[pre + "Wq"], Wk=I[pre + "Wk"], Wv=I[pre + "Wv"], Wo=I[pre + "Wo"],
                b=[I[pre + n] for n in ("bq", "bk", "bv")] if L == "B" else None,
                cos=rope_cos[0 if L == "A" else 1], sin=rope_sin[0 if L == "A" else 1])

        x_in = I["L0_attn_a_hidden_states"].rearrange("b s d -> (b s) d")
        out2 = out.rearrange("b s d -> (b s) d")
        A = layer("A", True, x_in, x1, "half")
        B = layer("B", False, x2, x3, "pairs")

        PIECES = [(kind, m, k) for m in range(3) for kind in ("wt", "mm") for k in range(2)] + [("vt", 2, 0), ("vt", 2, 1)]
        assert len(PIECES) == PJ_GROUP

        def apart(eng):
            eng.sem_inc(s0["apart"], 1)

        def att_sync(sp, L):
            s = L["s"]
            sp.dma_start(COS, L["cos"]).then_inc(s["tab"], 16)
            sp.dma_start(SIN, L["sin"]).then_inc(s["tab"], 16)
            if L["topk"]:
                sp.dma_start(small[:, 240:256], search_d).then_inc(s["tab"], 16)

            def weights(m, p, g):
                w = (L["Wq"], L["Wk"], L["Wv"])[m]
                sp.wait_ge(s["pj_full"], p * PJ_GROUP + (0, 2, 6)[m] + 1)
                apart(sp)
                if L["gqa"] and m:
                    for c in range(HG):
                        sp.dma_start(W_stage[HD * c:HD * c + HD, :], w[bass.ds(g * HD, HD), :]).then_inc(s["w"][m], 16)
                else:
                    sp.dma_start(W_stage[:, :], w[bass.ds(g * P, P), :]).then_inc(s["w"][m], 16)
                if L["bias"]:
                    bias = L["b"][m].rearrange("(n o) -> n o", o=1)
                    sp.dma_start(bias_st[:, m:m + 1], bias[bass.ds(g * P, P), :]).then_inc(s["w"][m], 16)

            with sp.Fori(0, BATCH) as b:
                for t in range(NT):
                    sp.dma_start(XL[:, t, :], L["src"][bass.ds(b * SEQ + t * P, P), :]).then_inc(s["xl"][t], 16)
                weights(0, b * NG, 0)
                with sp.Fori(0, NG - 1) as g:
                    weights(1, b * NG + g, g)
                    weights(2, b * NG + g, g)
                    weights(0, b * NG + g + 1, g + 1)
                weights(1, b * NG + NG - 1, NG - 1)
                weights(2, b * NG + NG - 1, NG - 1)
                if L["bias"]:
                    sp.wait_ge(s["pj_full"], (b + 1) * (NG * PJ_GROUP) + 1)
                    apart(sp)
                    sp.dma_start(bo_row, I["L0_attn_b_bo"].rearrange("(a n) -> a n", a=1)).then_inc(s["bo"], 16)
                sp.wait_ge(s["pv_full"], (b + 1) * (NG * NT))
                apart(sp)
                for ro in range(KT):
                    if ro >= 4:
                        sp.wait_ge(s["tr_full"], b * TR_BATCH + (TR_LN + NG * TR_GROUP + 2 * (ro - 3)))
                        apart(sp)
                    sp.dma_start(WO[:, ro % 4, :], L["Wo"][ro * P:ro * P + P, :]).then_inc(s["wo"][ro % 4], 16)
                for t in range(NT + 4):
                    if t >= 4:
                        sp.wait_ge(s["o_free"], b * NT + (t - 4) + 1 + 2)
                        apart(sp)
                        sp.dma_start(L["dst"][bass.ds(b * SEQ + (t - 4) * P, P), :],
                                     EX[:, t % 4, :]).then_inc(s["st"][t % 4], 16)
                    if t < NT:
                        if t >= 4:
                            sp.wait_ge(s["st"][t % 4], b * 32 + (s["slot0"] + 16))
                            apart(sp)
                        sp.dma_start(EX[:, t % 4, :], L["src"][bass.ds(b * SEQ + t * P, P), :]).then_inc(s["xo"][t % 4], 16)
                for k in range(4):
                    sp.wait_ge(s["st"][k], b * 32 + (s["slot0"] + 32))
                    apart(sp)

        def att_tensor(pe, L):
            s = L["s"]
            tr, pj = Tally(s["tr_full"]), Tally(s["pj_full"])
            pe.sem_inc(s["pj_full"], 1)

            def tr_slot():
                pe.wait_ge(s["tr_free"], tr.base + (tr.n + 1))
                return TR_ring[:, tr.n % 2, :]

            def piece(p, kind, m, k):
                pe.wait_ge(s["pj_free"], pj.base + (pj.n + 1))
                if kind == "wt":
                    if k == 0:
                        pe.wait_ge(s["w"][m], (p + 1) * (16 * ((HG if L["gqa"] and m else 1) + (1 if L["bias"] else 0))))
                    for c in range(4):
                        ins = pe.transpose(PJ[:, c * P:c * P + P], W_stage[:, (4 * k + c) * P:(4 * k + c + 1) * P],
                                           ident[:, :])
                    pj.mark(ins)
                elif kind == "mm":
                    for kt in range(KT):
                        ins = pe.matmul(PJ[:, :], WT[:, kt, :], XT[:, kt, k * 512:k * 512 + 512],
                                        start=(kt == 0), stop=(kt == KT - 1))
                    pj.mark(ins)
                else:
                    for c in range(4):
                        t = 4 * k + c
                        ins = pe.transpose(PJ[:, c * P:c * P + P], VT[:, t * P:t * P + P], ident[:, :])
                    pj.mark(ins)

            def scores(it, i, heads=range(HG)):
                n = (i + 1) * P
                for h in heads:
                    x = i * HG + h
                    pe.wait_ge(s["s_free"], it * (NT * HG) + (x + 1))
                    q, keys = QS[0:3 * HD, h, i * P:i * P + P], L["KS"][0:3 * HD, h % L["key_heads"], :]
                    for c in range(0, n, 512):
                        w = min(512, n - c)
                        last = c + w == n
                        pe.matmul(S_ring[:, x % 2, c:c + w], q, keys[:, c:c + w],
                                  start=True, stop=not last)
                    pe.matmul(S_ring[:, x % 2, n - P:n], ident16[:, :], future16[:, :],
                              start=False, stop=True).then_inc(s["s_full"], 1)

            def attention(it, g, project):
                pe.wait_ge(s["stacked"], (it + 1) * 2 * HG)
                apart(pe)
                pe.wait_ge(s["stacked_k"], (it + 1) * 2 * L["key_heads"])
                apart(pe)
                pe.wait_ge(s["stacked_low"], (it + 1) * (HG + L["key_heads"]))
                scores(it, 0)
                for i in range(NT):
                    searched = L["topk"] and i > 0
                    if i + 1 < NT and not searched:
                        scores(it, i + 1)
                    if project:
                        for j in UNIT_PIECES[L["topk"]][i]:
                            piece(it + 1, *PIECES[j])
                    if searched:
                        if i + 1 < NT:
                            scores(it, i + 1, (0, 1))
                        pe.wait_ge(s["good"], it * (NT - 1) + i)
                        pe.matmul(PV[0:1, 504:504 + HG], ones[:, 0:1], good, start=True, stop=True).then_inc(s["flag"], 1)
                        if i + 1 < NT:
                            scores(it, i + 1, (2, 3))
                    for h in range(HG):
                        if L["topk"] and i:
                            pe.wait_ge(s["p_ready"], it * (HG * (NT - 1)) + ((i - 1) * HG + h + 1))
                        else:
                            pe.wait_ge(s["e_ready"], it * (HG * NT) + (i * HG + h + 1))
                        for c in range(0, i + 1, 4):
                            slot = tr_slot()
                            for kt in range(c, min(c + 4, i + 1)):
                                ins = pe.transpose(slot[:, (kt - c) * P:(kt - c + 1) * P],
                                                   EX[:, h, kt * P:kt * P + P], ident[:, :])
                            tr.mark(ins)
                    pe.wait_ge(s["tr_free"], tr.base + (tr.n + 2))
                    pe.wait_ge(s["pv_free"], it * NT + (i + 1))
                    if i == 0:
                        pe.wait_ge(s["handoff"], it + 1)
                    for kt in range(i + 1):
                        for h in range(HG):
                            ins = pe.matmul(PV[HD * h:HD * h + HD, 0:P], CUR_V[:, kt, HD * h:HD * h + HD],
                                            PT[:, h * NT + kt, :], start=(kt == 0), stop=(kt == i))
                    ins.then_inc(s["pv_full"], 1)
                    slot = tr_slot()
                    pe.wait_ge(s["rinv_ready"], it * NT + (i + 1))
                    tr.mark(pe.matmul(slot[:, 0:P], rinv, ident[:, :],
                                        start=True, stop=True))

            with pe.Fori(0, BATCH) as b:
                tr.at(b * TR_BATCH)
                pj.at(b * (PJ_GROUP * NG))
                for t in range(NT):
                    pe.wait_ge(s["x_norm"], b * NT + (t + 1))
                    for k in range(2):
                        slot = tr_slot()
                        for c in range(4):
                            ins = pe.transpose(slot[:, c * P:c * P + P], XL[:, t, (4 * k + c) * P:(4 * k + c + 1) * P],
                                               ident[:, :])
                        tr.mark(ins)
                pe.wait_ge(s["tr_free"], tr.base + (tr.n + 2))
                pe.wait_ge(s["o_free"], b * NT + 2)
                for q in PIECES:
                    piece(b * NG, *q)
                with pe.Fori(0, NG - 1) as g:
                    tr.at(b * TR_BATCH + TR_LN + g * TR_GROUP)
                    pj.at(b * (PJ_GROUP * NG) + PJ_GROUP + g * PJ_GROUP)
                    attention(b * NG + g, g, True)
                    assert tr.n == TR_GROUP and pj.n == PJ_GROUP
                tr.at(b * TR_BATCH + TR_LN + (NG - 1) * TR_GROUP)
                attention(b * NG + NG - 1, NG - 1, False)
                WoT = S_sb.rearrange("p a h n -> p (a h) n")
                for ro in range(KT):
                    pe.wait_ge(s["wo"][ro % 4], b * 32 + (s["slot0"] + 16 + 16 * (ro // 4)))
                    for k in range(2):
                        slot = tr_slot()
                        for c in range(4):
                            ins = pe.transpose(slot[:, c * P:c * P + P], WO[:, ro % 4, (4 * k + c) * P:(4 * k + c + 1) * P],
                                               ident[:, :])
                        tr.mark(ins)
                pe.wait_ge(s["tr_free"], tr.base + (tr.n + 2))
                pe.wait_ge(s["s_free"], (b + 1) * (NG * NT * HG) + 2)
                pe.wait_ge(s["pv_free"], (b + 1) * (NG * NT) + 1)
                if L["bias"]:
                    pe.wait_ge(s["bo"], b * 16 + 16)
                for t in range(NT):
                    pe.wait_ge(s["o_free"], b * NT + (t + 1))
                    for c in range(2):
                        for kt in range(KT):
                            ins = pe.matmul(S_ring[:, t % 2, c * 512:c * 512 + 512], OT[:, kt, t * P:t * P + P],
                                            WoT[:, kt, c * 512:c * 512 + 512], start=(kt == 0),
                                            stop=(kt == KT - 1 and not L["bias"]))
                        if L["bias"]:
                            ins = pe.matmul(S_ring[:, t % 2, c * 512:c * 512 + 512], ones[0:1, :],
                                            bo_row[0:1, c * 512:c * 512 + 512], start=False, stop=True)
                    ins.then_inc(s["o_full"], 1)

        def att_scalar(act, L):
            s = L["s"]
            tr, pj = Tally(s["tr_free"]), Tally(s["pj_free"])
            act.sem_inc(s["tr_free"], 2)
            act.sem_inc(s["pj_free"], 1)

            def tr_out(dst, cols=512, split=4):
                act.wait_ge(s["tr_full"], tr.base + (tr.n + 1))
                src = TR_ring[:, tr.n % 2, 0:cols]
                if split:
                    src = src.rearrange("p (c n) -> p c n", n=P)
                tr.mark(act.copy(dst, src))

            def piece(kind, m, k):
                act.wait_ge(s["pj_full"], pj.base + (pj.n + 2))
                if kind == "wt":
                    pj.mark(act.copy(WT[:, 4 * k:4 * k + 4, :], PJ[:, :].rearrange("p (c n) -> p c n", n=P)))
                elif kind == "mm":
                    dst = (VT if m == 2 else NXT[:, m, :])[:, k * 512:k * 512 + 512]
                    if L["bias"]:
                        pj.mark(act.activation(dst, PJ[:, :], ACT.Identity, bias=bias_st[:, m:m + 1]))
                    else:
                        pj.mark(act.copy(dst, PJ[:, :]))
                else:
                    pj.mark(act.copy(NXV[:, 4 * k:4 * k + 4, :], PJ[:, :].rearrange("p (c n) -> p c n", n=P)))

            def stack_high_q(p1, heads):
                act.wait_ge(s["roped"], p1 * 2 + 1)
                act.wait_ge(s["s_free"], p1 * (NT * HG) + 2)
                for h in heads:
                    for r in (0, 2):
                        act.copy(QS[HD * r:HD * r + HD, h, :], SH[HD * h:HD * h + HD, 0, :]).then_inc(s["stacked"], 1)

            def stack_high_k(p1):
                act.wait_ge(s["roped"], p1 * 2 + 2)
                for r in (0, 1):
                    act.copy(KS_A[HD * r:HD * r + HD, 0, :], SH[0:HD, 1, :]).then_inc(s["stacked_k"], 1)

            def exps(it, i):
                n = (i + 1) * P
                act.wait_ge(s["nb_ready"], it * NT + (i + 1))
                act.wait_ge(s["s_free"], it * (NT * HG) + (i * HG + HG + 2))
                for h in range(HG):
                    if L["topk"] and i:
                        ins = act.activation(EX[:, h, 0:n], S_sb[:, i % 2, h, 0:n], ACT.Exp,
                                             bias=nb[:, i % 2, h:h + 1], scale=EXP_SCALE)
                    else:
                        ins = act.activation(EX[:, h, 0:n], S_sb[:, i % 2, h, 0:n], ACT.Exp,
                                             bias=nb[:, i % 2, h:h + 1], scale=EXP_SCALE,
                                             accum_out=sums[:, i % 2, h:h + 1])
                    ins.then_inc(s["e_ready"], 1)

            def probs_out(i, heads):
                for h in heads:
                    for c in range(0, i + 1, 4):
                        w = min(4, i + 1 - c)
                        tr_out(PT[:, h * NT + c:h * NT + c + w, :], cols=w * P)

            def count(it, i, k):
                n = (i + 1) * P
                act.wait_ge(s["t_new"], it * ((NT - 1) * NC) + ((i - 1) * NC + k + 1))
                for h in ACT_HEADS:
                    act.activation(SEL[:, h, 0:n], S_sb[:, i % 2, h, 0:n], ACT.Sign, bias=points[:, k % 3, h, 1:2],
                                   scale=-1.0, accum_out=act_sum[:, h - 2:h - 1]).then_inc(s["counted"], 1)

            def attention(it, project):
                for i in range(NT):
                    n = (i + 1) * P
                    pieces = [PIECES[j] for j in UNIT_PIECES[L["topk"]][i]] if project else []
                    if L["topk"] and i:
                        for k in range(NC):
                            count(it, i, k)
                            if project and i == NT - 1:
                                if k < HG:
                                    stack_high_q(it + 1, (k,))
                                else:
                                    stack_high_k(it + 1)
                            if k < 2:
                                probs_out(i - 1, (2 * k, 2 * k + 1))
                            if k == 3:
                                tr_out(Rsb, cols=P, split=0)
                        for q in pieces[:-1]:
                            piece(*q)
                        act.wait_ge(s["below"], it * ((NT - 1) * 2) + i * 2)
                        for h in ACT_HEADS:
                            act.activation(EX[:, h, 0:n], SEL[:, h, 0:n], ACT.Sign, bias=half,
                                           accum_out=act_sum[:, h - 2:h - 1]).then_inc(s["counted"], 1)
                        act.wait_ge(s["counted"], it * ((NT - 1) * 2 * (NC + 1)) + i * 2 * (NC + 1))
                        exps(it, i)
                        for q in pieces[-1:]:
                            piece(*q)
                    else:
                        if i:
                            probs_out(i - 1, range(HG))
                        exps(it, i)
                        if i:
                            tr_out(Rsb, cols=P, split=0)
                        for q in pieces:
                            piece(*q)
                        if project and i == NT - 2:
                            stack_high_q(it + 1, range(HG))
                probs_out(NT - 1, range(HG))
                tr_out(Rsb, cols=P, split=0)

            with act.Fori(0, BATCH) as b:
                tr.at(b * TR_BATCH)
                pj.at(b * (PJ_GROUP * NG))
                act.wait_ge(s["ln_var"], b + 1)
                act.activation(ln_sd[:, 0:NT], ln_ve[:, 0:NT], ACT.Sqrt).then_inc(s["ln_sd"], 1)
                for t in range(NT):
                    for k in range(2):
                        tr_out(XT[:, 4 * k:4 * k + 4, t * P:t * P + P])
                for q in PIECES:
                    piece(*q)
                stack_high_q(b * NG, range(HG))
                if L["gqa"]:
                    stack_high_k(b * NG)
                with act.Fori(0, NG - 1) as g:
                    tr.at(b * TR_BATCH + TR_LN + g * TR_GROUP)
                    pj.at(b * (PJ_GROUP * NG) + PJ_GROUP + g * PJ_GROUP)
                    attention(b * NG + g, True)
                tr.at(b * TR_BATCH + TR_LN + (NG - 1) * TR_GROUP)
                attention(b * NG + NG - 1, False)
                WoT = S_sb.rearrange("p a h n -> p (a h) n")
                for ro in range(KT):
                    for k in range(2):
                        tr_out(WoT[:, 4 * k:4 * k + 4, ro * P:ro * P + P])
                assert tr.n == TR_GROUP + TR_WO

        def layer_norm(dve, s, chain, n_tiles, b1, load_wait, tile, write):
            for t in range(n_tiles):
                load_wait(t)
                x = tile(t)
                if t:
                    chain.reached(dve)
                chain.mark(dve.bn_stats(ln_st[:, 0, :], x[:, 0:512]))
                chain.mark(dve.bn_stats(ln_st[:, 1, :], x[:, 512:1024]))
                chain.reached(dve)
                apart(dve)
                chain.mark(dve.bn_aggr(ln_mv[:, t, :], ln_st))
            chain.reached(dve)
            dve.tensor_scalar(ln_ve[:, 0:n_tiles], ln_mv[:, 0:n_tiles, 1], LN_EPS, None, ALU.add).then_inc(s["ln_var"], 1)
            dve.wait_ge(s["ln_sd"], b1)
            r, tt, ve = ln_r[:, 0:n_tiles], ln_t[:, 0:n_tiles], ln_ve[:, 0:n_tiles]
            chain.mark(dve.reciprocal(r, ln_sd[:, 0:n_tiles]))
            chain.reached(dve)
            chain.mark(dve.tensor_tensor(tt, ve, r, ALU.mult))
            chain.reached(dve)
            chain.mark(dve.tensor_tensor(tt, tt, r, ALU.mult))
            chain.reached(dve)
            chain.mark(dve.tensor_scalar(tt, tt, -0.5, 1.5, ALU.mult, ALU.add))
            chain.reached(dve)
            chain.mark(dve.tensor_tensor(r, r, tt, ALU.mult))
            chain.reached(dve)
            for t in range(n_tiles):
                write(t)

        CH_LN = 3 * NT + 5
        CH_UNIT = 76

        def att_vector(dve, L):
            s = L["s"]
            ch = Tally(s["chain"])
            per_group = NT + (CH_UNIT * (NT - 1) if L["topk"] else 0)
            per_batch = CH_LN + NG * per_group
            dve.sem_inc(s["pv_free"], 1)
            dve.sem_inc(s["s_free"], 2)
            dve.sem_inc(s["o_free"], 2)

            def finalize(it, g, i):
                dve.wait_ge(s["pv_full"], it * NT + (i + 1))
                dve.wait_ge(s["tr_free"], ring_base[0] + (sum(TR_UNIT[:i + 1]) + 2))
                dve.tensor_tensor(OT[:, g, i * P:i * P + P], PV[:, 0:P], Rsb, ALU.mult).then_inc(s["pv_free"], 1)

            def shuffle(p1, m):
                dve.wait_ge(s["pj_free"], p1 * PJ_GROUP + (4 * m + 4 + 1))
                apart(dve)
                dve.stream_shuffle(SH[:, m, :], NXT[:, m, :], QK_ROPE[L["rope"]]).then_inc(s["shuffled"], 1)

            ring_base = [0]

            def step(ins):
                ch.mark(ins)
                ch.reached(dve)

            def scores_out(it, i):
                n = (i + 1) * P
                for h in range(HG):
                    x = i * HG + h
                    dve.wait_ge(s["s_full"], it * (NT * HG) + (x + 1))
                    dve.tensor_scalar(S_sb[:, i % 2, h, 0:n], S_ring[:, x % 2, 0:n], 1.0, -1.0, ALU.mult, ALU.max,
                                      accum_out=mx[:, i % 2, h:h + 1]).then_inc(s["s_free"], 1)
                dve.wait_ge(s["s_free"], it * (NT * HG) + (i * HG + HG + 2))
                dve.tensor_scalar(nb[:, i % 2, :], mx[:, i % 2, :], -EXP_SCALE, None, ALU.mult).then_inc(s["nb_ready"], 1)

            def statistics(it, i):
                every = max(1, i // 2)
                for h in range(HG):
                    ch.mark(dve.bn_stats(st6[:, h, :], S_sb[:, i % 2, h, 0:i * P:every]))
                ch.reached(dve)
                apart(dve)
                for h in range(HG):
                    ins = dve.bn_aggr(mv[:, h, :], st6[:, h, :])
                    if h + 1 < HG:
                        ch.mark(ins)
                    else:
                        ins.then_inc(s["stats"], 1)

            def first_threshold(it, i):
                dve.wait_ge(s["sd"], it * (NT - 1) + i)
                ch.mark(dve.tensor_scalar(slope, sd, slope_tab[:, i:i + 1], None, ALU.mult))
                dve.scalar_tensor_tensor(out=points[:, 0, :, 1], in0=sd, scalar=z_tab[:, i:i + 1], in1=mv[:, :, 0],
                                         op0=ALU.mult, op1=ALU.add).then_inc(s["t_new"], 1)

            def search_step(it, i, k):
                n = (i + 1) * P
                N, Q = points[:, k % 3], points[:, (k - 1) % 3]
                t_next = points[:, (k + 1) % 3, :, 1]
                e, t = N[:, :, 0], N[:, :, 1]
                dve.wait_ge(s["t_new"], it * ((NT - 1) * NC) + ((i - 1) * NC + k + 1))
                for h in range(HG):
                    if h not in ACT_HEADS:
                        ch.mark(dve.tensor_scalar(SEL[:, h, 0:n], S_sb[:, i % 2, h, 0:n], N[:, h, 1:2], -AIM,
                                                  ALU.is_ge, ALU.add, accum_out=N[:, h, 0:1]))
                signs_to_counts(it, i, k, N[:, 2:4, 0])
                if k == 0:
                    step(dve.tensor_scalar(tmp[:, 0, :], e, 0.0, 2 * STEP_OVER, ALU.is_ge, ALU.mult))
                    step(dve.scalar_tensor_tensor(out=tmp[:, 0, :], in0=tmp[:, 0, :], scalar=-STEP_OVER, in1=e,
                                                  op0=ALU.add, op1=ALU.add))
                    step(dve.tensor_tensor(tmp[:, 0, :], tmp[:, 0, :], slope, ALU.mult))
                    dve.tensor_tensor(t_next, t, tmp[:, 0, :], ALU.add).then_inc(s["t_new"], 1)
                    ch.mark(dve.tensor_copy(anchor, N))
                    ch.mark(dve.tensor_copy(G[:, :, 0:2], N))
                else:
                    if k >= 2 and k + 1 < NC:
                        step(dve.scalar_tensor_tensor(out=tmp[:, 1, :], in0=e, scalar=0.0, in1=tmp[:, 3, :],
                                                      op0=ALU.is_lt, op1=ALU.not_equal))
                        apart(dve)
                        step(dve.copy_predicated(anchor, tmp[:, 1, :].bitcast(I32).unsqueeze(2).to_broadcast([P, HG, 2]), Q))
                    if k + 1 < NC:
                        ch.mark(dve.scalar_tensor_tensor(out=tmp[:, 1, :], in0=anchor[:, :, 0], scalar=0.1, in1=e,
                                                         op0=ALU.add, op1=ALU.subtract))
                        step(dve.tensor_tensor(tmp[:, 0, :], anchor[:, :, 1], t, ALU.subtract))
                        ch.mark(dve.reciprocal(tmp[:, 2, :], tmp[:, 1, :]))
                        step(dve.tensor_tensor(tmp[:, 0, :], tmp[:, 0, :], e, ALU.mult))
                        step(dve.tensor_tensor(tmp[:, 0, :], tmp[:, 0, :], tmp[:, 2, :], ALU.mult))
                        dve.tensor_tensor(t_next, t, tmp[:, 0, :], ALU.subtract).then_inc(s["t_new"], 1)
                    if 0 < k < NC - 2:
                        ch.mark(dve.tensor_scalar(tmp[:, 3, :], e, 0.0, None, ALU.is_lt))
                    step(dve.tensor_tensor(tmp[:, 4, :], e, e, ALU.mult))
                    step(dve.tensor_scalar(tmp[:, 4, :], tmp[:, 4, :], (TOP - AIM) ** 2 + 0.5, None, ALU.is_le))
                    apart(dve)
                    ch.mark(dve.copy_predicated(G[:, :, 0:2],
                                                tmp[:, 4, :].bitcast(I32).unsqueeze(2).to_broadcast([P, HG, 2]), N))

            def signs_to_counts(it, i, k, out):
                dve.wait_ge(s["counted"], it * ((NT - 1) * 2 * (NC + 1)) + ((i - 1) * 2 * (NC + 1) + 2 * k + 2))
                step(dve.tensor_scalar(out, act_sum, -0.5, (i + 1) * P / 2 - AIM, ALU.mult, ALU.add))

            def settle(it, i):
                n = (i + 1) * P
                ch.reached(dve)
                for h in (2, 3, 0, 1):
                    ins = dve.scalar_tensor_tensor(out=SEL[:, h, 0:n], in0=S_sb[:, i % 2, h, 0:n], scalar=G[:, h, 1:2],
                                                   in1=S_sb[:, i % 2, h, 0:n], op0=ALU.is_ge, op1=ALU.subtract, reverse1=True)
                    if h in ACT_HEADS:
                        ins.then_inc(s["below"], 1)
                    else:
                        ch.mark(ins)
                dve.wait_ge(s["below"], it * ((NT - 1) * 2) + i * 2)
                ch.reached(dve)
                apart(dve)
                for h in (2, 3, 0, 1):
                    ch.mark(dve.max(G[:, h, 2:10], SEL[:, h, 0:n]))
                signs_to_counts(it, i, NC, G[:, 2:4, 0])
                step(dve.tensor_scalar(tmp[:, 0, :], G[:, :, 0], -1.0, TOP - AIM, ALU.mult, ALU.add))
                step(dve.tensor_tensor(OH, tmp[:, 0, :].unsqueeze(2).to_broadcast([P, HG, 8]),
                                       iota[:, :].unsqueeze(1).to_broadcast([P, HG, 8]), ALU.is_equal))
                for dst, at in ((tstar, 1), (tnext, 2)):
                    step(dve.tensor_tensor(PR, OH, G[:, :, at:at + 8], ALU.mult))
                    step(dve.tensor_reduce(dst, PR, mybir.AxisListType.X, ALU.add))
                dve.tensor_tensor(good, tstar, tnext, ALU.is_gt).then_inc(s["good"], 1)

            def repair(it, i):
                n = (i + 1) * P
                dve.wait_ge(s["flag"], it * (NT - 1) + i)
                step(dve.tensor_reduce(small[0:1, 106:107], PV[0:1, 504:504 + HG], mybir.AxisListType.X, ALU.add))
                step(dve.tensor_copy(ended_well[0:1, :], small[0:1, 106:107]))
                apart(dve)
                rows = dve.value_load(ended_well[0:1, :])
                with dve.If(rows != HG * P):
                    for h in range(HG):
                        dve.max(m8[:, h, :], S_sb[:, i % 2, h, 0:n])
                        dve.drain()
                        dve.match_replace(SEL[:, h, 0:n], m8[:, h, :], S_sb[:, i % 2, h, 0:n], TAKEN)
                        dve.drain()
                        with dve.Fori(0, TOP // 8 - 1):
                            dve.max(m8[:, h, :], SEL[:, h, 0:n])
                            dve.drain()
                            dve.match_replace(SEL[:, h, 0:n], m8[:, h, :], SEL[:, h, 0:n], TAKEN)
                            dve.drain()
                        dve.tensor_scalar(S_sb[:, i % 2, h, 0:n], SEL[:, h, 0:n], TAKEN / 2, None, ALU.is_le)
                    dve.memset(tstar, 0.5)
                    dve.drain()

            def stack_high_k(p1):
                dve.wait_ge(s["roped"], p1 * 2 + 2)
                apart(dve)
                dve.wait_ge(s["s_free"], p1 * (NT * HG) + 2)
                for h in range(HG):
                    for r in (0, 1):
                        dve.tensor_copy(KS_B[HD * r:HD * r + HD, h, :], SH[HD * h:HD * h + HD, 1, :]).then_inc(s["stacked_k"], 1)

            def attention(it, b, g, project):
                ring_base[0] = b * TR_BATCH + TR_LN + g * TR_GROUP
                dve.wait_ge(s["pj_free"], it * PJ_GROUP + (PJ_GROUP + 1))
                dve.tensor_copy(CUR_V, NXV).then_inc(s["handoff"], 1)
                scores_out(it, 0)
                for i in range(NT):
                    n = (i + 1) * P
                    searched = L["topk"] and i > 0
                    if searched:
                        if project and i in ROTATED_AT[L["topk"]]:
                            shuffle(it + 1, ROTATED_AT[L["topk"]].index(i))
                        for k in range(NC):
                            search_step(it, i, k)
                        finalize(it, g, i - 1)
                        settle(it, i)
                    if i + 1 < NT:
                        scores_out(it, i + 1)
                        if L["topk"]:
                            statistics(it, i + 1)
                    if i and not searched:
                        finalize(it, g, i - 1)
                        if project and i in ROTATED_AT[L["topk"]]:
                            shuffle(it + 1, ROTATED_AT[L["topk"]].index(i))
                    dve.wait_ge(s["e_ready"], it * (HG * NT) + (i * HG + HG))
                    if searched:
                        apart(dve)
                        repair(it, i)
                    if L["topk"] and i + 1 < NT:
                        first_threshold(it, i + 1)
                    if searched:
                        for h in range(HG):
                            dve.scalar_tensor_tensor(out=EX[:, h, 0:n], in0=S_sb[:, i % 2, h, 0:n], scalar=tstar[:, h:h + 1],
                                                     in1=EX[:, h, 0:n], op0=ALU.is_ge, op1=ALU.mult,
                                                     accum_out=sums[:, i % 2, h:h + 1]).then_inc(s["p_ready"], 1)
                        dve.wait_ge(s["p_ready"], it * (HG * (NT - 1)) + i * HG)
                    step(dve.reciprocal(rsum, sums[:, i % 2, :]))
                    dve.tensor_copy(rinv.rearrange("p (h d) -> p h d", h=HG),
                                    rsum.unsqueeze(2).to_broadcast([P, HG, HD])).then_inc(s["rinv_ready"], 1)
                    if project and not L["gqa"] and i == NT - 2:
                        stack_high_k(it + 1)
                finalize(it, g, NT - 1)

            with dve.Fori(0, BATCH) as b:
                ch.at(b * per_batch)

                def norm(t):
                    dve.tensor_scalar(XL[:, t, :], XL[:, t, :], ln_mv[:, t, 0:1], ln_r[:, t:t + 1], ALU.subtract,
                                      ALU.mult).then_inc(s["x_norm"], 1)

                layer_norm(dve, s, ch, NT, b + 1, lambda t: dve.wait_ge(s["xl"][t], b * 16 + (s["xl0"] + 16)), lambda t: XL[:, t, :],
                           norm)
                assert ch.n == CH_LN, ch.n
                for m in range(2):
                    shuffle(b * NG, m)
                if not L["gqa"]:
                    stack_high_k(b * NG)
                with dve.Fori(0, NG - 1) as g:
                    ch.at(b * per_batch + CH_LN + g * per_group)
                    attention(b * NG + g, b, g, True)
                    assert ch.n == per_group, (ch.n, per_group)
                ch.at(b * per_batch + CH_LN + (NG - 1) * per_group)
                attention(b * NG + NG - 1, b, NG - 1, False)
                for t in range(NT):
                    dve.wait_ge(s["o_full"], b * NT + (t + 1))
                    dve.wait_ge(s["xo"][t % 4], b * 32 + (s["slot0"] + 16 + 16 * (t // 4)))
                    dve.tensor_tensor(EX[:, t % 4, :], EX[:, t % 4, :], S_ring[:, t % 2, :],
                                      ALU.add).then_inc(s["o_free"], 1)

        def att_pool(pool, L):
            s = L["s"]

            def rope(p1, m):
                pool.wait_ge(s["shuffled"], p1 * 2 + (m + 1))
                x, sh = NXT[:, m, :], SH[:, m, :]
                pool.tensor_tensor(sh, sh, SIN, ALU.mult).then_inc(s["rope_step"], 1)
                pool.tensor_tensor(x, x, COS, ALU.mult).then_inc(s["rope_step"], 1)
                pool.wait_ge(s["rope_step"], p1 * 6 + (3 * m + 2))
                pool.tensor_tensor(x, x, sh, ALU.add).then_inc(s["rope_step"], 1)
                pool.wait_ge(s["rope_step"], p1 * 6 + (3 * m + 3))
                apart(pool)
                pool.tensor_copy(sh.bitcast(F32R), x).then_inc(s["roped"], 1)

            def stack_low(p1):
                pool.wait_ge(s["roped"], p1 * 2 + 2)
                apart(pool)
                pool.wait_ge(s["s_free"], p1 * (NT * HG) + 2)
                n = p1 * (HG + L["key_heads"])
                for h in range(HG):
                    pool.tensor_tensor(QS[HD:2 * HD, h, :], NXT[HD * h:HD * h + HD, 0, :], SH[HD * h:HD * h + HD, 0, :],
                                       ALU.subtract).then_inc(s["stacked_low"], 1)
                    pool.wait_ge(s["stacked_low"], n + (h + 1))
                for h in range(L["key_heads"]):
                    pool.tensor_tensor(L["KS"][2 * HD:3 * HD, h, :], NXT[HD * h:HD * h + HD, 1, :],
                                       SH[HD * h:HD * h + HD, 1, :], ALU.subtract).then_inc(s["stacked_low"], 1)
                    pool.wait_ge(s["stacked_low"], n + (HG + h + 1))
                apart(pool)

            def attention(it, project):
                for i in range(1, NT):
                    if project and i - 1 in ROTATED_AT[L["topk"]]:
                        rope(it + 1, ROTATED_AT[L["topk"]].index(i - 1))
                    if L["topk"]:
                        pool.wait_ge(s["stats"], it * (NT - 1) + i)
                        pool.tensor_tensor(sd, mv[:, :, 1], one_half, ALU.pow).then_inc(s["sd"], 1)
                if project:
                    if L["topk"]:
                        pool.wait_ge(s["sd"], (it + 1) * (NT - 1))
                        apart(pool)
                    stack_low(it + 1)

            pool.wait_ge(s["tab"], 48 if L["topk"] else 32)
            with pool.Fori(0, BATCH) as b:
                for m in range(2):
                    rope(b * NG, m)
                stack_low(b * NG)
                with pool.Fori(0, NG - 1) as g:
                    attention(b * NG + g, True)
                attention(b * NG + NG - 1, False)

        take = carve()
        FX = take(NTOK, DM)
        NCOL = DM + HID + E * R
        FW = take(KT, NCOL)
        F_stage = take(4, DM)
        F_gw1 = take(DM)
        F_B = take(DM)
        F_xn = take(2, DM)
        F_xT = take(2, KT, P)
        F_tmp = take(NTOK, P)
        F_h = take(NTOK, HID)
        F_h2 = take(NTOK, HID)
        F_hT = take(NTOK, P)
        F_tT = F_hT
        F_g = take(NTOK, E)
        F_top = take(NTOK, E)
        F_idx = take(NTOK, E)
        F_oh = take(NTOK, 2, E)
        F_w = take(NTOK, E)
        F_w2 = take(NTOK, E)
        F_cnt = take(2 * E)
        F_p = take(NTOK, 4)
        F_mu = take(NTOK)
        F_va = take(NTOK)
        F_vb = take(NTOK)
        F_row = take(4, HID)
        F_gw2T = take(E)
        fsmall = take(512)
        f_st = fsmall[:, 0:12].rearrange("p (a b) -> p a b", a=2)
        f_mv = fsmall[:, 16:48].rearrange("p (t c) -> p t c", c=2)
        f_ve, f_sd, f_r, f_t = (fsmall[:, 64 + 16 * k:80 + 16 * k] for k in range(4))

        def ffn_layer(n, src, dst):
            s = dict(**{q: sem(f"F{n}_{q}") for q in (
                      "ln_var", "ln_sd", "x_norm", "tr_full", "tr_free", "m_full", "m_free", "a_full", "a_free", "w2",
                      "h_ln", "h_sd", "chain", "h_ready", "gates", "exp_in", "exp_out", "oh", "cnt", "t_ready", "l_full",
                      "l_done", "st", "loraA", "gw1", "misc", "h_in")})
            s["x"], s["wl"] = dma["fx"], dma["fw"]
            s["x0"], s["wl0"] = (0, 0) if n == 1 else (64, 32)
            return dict(s=s, src=src, dst=dst)

        F1 = ffn_layer(1, x1, x2)
        F2 = ffn_layer(2, x3, out2)
        FPRE = "L0_ffn_"

        def ffn_sync(sp, F):
            s = F["s"]
            def x_in(k):
                for t in range(4 * k, 4 * k + 4):
                    sp.dma_start(FX[:, t, :], F["src"][t * P:t * P + P, :]).then_inc(s["x"][k], 16)

            for ro in range(KT):
                if ro == 4:
                    x_in(0)
                    x_in(1)
                if ro >= 4:
                    sp.wait_ge(s["tr_full"], 2 * (ro - 3))
                sp.dma_start(F_stage[:, ro % 4, :], I[FPRE + "weight"][ro * P:ro * P + P, :]).then_inc(s["wl"][ro % 4], 16)
            x_in(2)
            x_in(3)
            sp.dma_start(F_gw1[0:HID, :], I[FPRE + "gw1"]).then_inc(s["gw1"], 16)
            for e in range(E):
                for kt in range(KT):
                    sp.dma_start(FW[:, kt, DM + HID + e * R:DM + HID + e * R + R],
                                 I[FPRE + "lora_A"][e, kt * P:kt * P + P, :]).then_inc(s["loraA"], 16)
            sp.dma_start(F_B, I[FPRE + "lora_B"].rearrange("e r o -> (e r) o")).then_inc(s["misc"], 16)
            for k, nme in enumerate(("gb1", "ln_gamma", "ln_beta", "gb2")):
                w = HID if k < 3 else E
                sp.dma_start(F_row[:, k, 0:w], I[FPRE + nme].partition_broadcast(P)).then_inc(s["misc"], 16)
            sp.dma_start(F_gw2T[0:HID, :], I[FPRE + "gw2"].rearrange("e f -> f e"),
                         allow_slow_non_contiguous=True).then_inc(s["misc"], 16)
            for t in range(NTOK):
                sp.wait_ge(s["l_done"], t + 1)
                sp.dma_start(F["dst"][t * P:t * P + P, :], FX[:, t, :]).then_inc(s["st"], 16)
            sp.wait_ge(s["st"], 16 * NTOK)

        N_MISC = 6
        T_W = 2 * KT + 2

        def ffn_tensor(pe, F):
            s = F["s"]
            tr = Tally(s["tr_full"])

            def tr_slot():
                pe.wait_ge(s["tr_free"], tr.base + (tr.n + 1))
                return TR_ring[:, tr.n % 2, :]

            for ro in range(KT):
                pe.wait_ge(s["wl"][ro % 4], s["wl0"] + 16 * (1 + ro // 4))
                for k in range(2):
                    slot = tr_slot()
                    for c in range(4):
                        ins = pe.transpose(slot[:, c * P:c * P + P],
                                           F_stage[:, ro % 4, (4 * k + c) * P:(4 * k + c + 1) * P], ident[:, :])
                    tr.mark(ins)
            pe.wait_ge(s["gw1"], 16)
            for k in range(2):
                slot = tr_slot()
                for c in range(4):
                    kt = 4 * k + c
                    ins = pe.transpose(slot[:, c * HID:c * HID + HID], F_gw1[0:HID, kt * P:kt * P + P],
                                       ident[0:HID, 0:HID])
                tr.mark(ins)
            pe.wait_ge(s["tr_free"], tr.base + (tr.n + 2))
            pe.wait_ge(s["loraA"], 16 * E * KT)
            with pe.Fori(0, NTOK // 2) as tp:
                tr.at(tp * 4 + T_W)
                for q in range(2):
                    pe.wait_ge(s["x_norm"], tp * 2 + (q + 1))
                    for k in range(2):
                        slot = tr_slot()
                        for c in range(4):
                            ins = pe.transpose(slot[:, c * P:c * P + P], F_xn[:, q, (4 * k + c) * P:(4 * k + c + 1) * P],
                                               ident[:, :])
                        tr.mark(ins)
                    pe.wait_ge(s["tr_free"], tr.base + (tr.n + 2))
                    pe.wait_ge(s["m_free"], tp * 2 + (q + 1))
                    pe.wait_ge(s["a_free"], tp * 2 + (q + 1))
                    aux = (PJ, PV)[q]
                    for kt in range(KT):
                        for c in range(2):
                            ins = pe.matmul(S_ring[:, q, c * 512:c * 512 + 512], F_xT[:, q, kt, :],
                                            FW[:, kt, c * 512:c * 512 + 512], start=(kt == 0), stop=(kt == KT - 1))
                        if kt == KT - 1:
                            ins.then_inc(s["m_full"], 1)
                        ins = pe.matmul(aux[:, 0:HID + E * R], F_xT[:, q, kt, :], FW[:, kt, DM:NCOL],
                                        start=(kt == 0), stop=(kt == KT - 1))
                    ins.then_inc(s["a_full"], 1)
            tr.at(4 * (NTOK // 2) + T_W)
            pe.wait_ge(s["h_ready"], 1)
            for c in range(4):
                slot = tr_slot()
                for t in range(4 * c, 4 * c + 4):
                    ins = pe.transpose(slot[0:HID, (t % 4) * P:(t % 4 + 1) * P], F_h[:, t, :], ident[:, :])
                tr.mark(ins)
            pe.wait_ge(s["tr_free"], tr.base + (tr.n + 2))
            pe.wait_ge(s["misc"], 16 * N_MISC)
            pe.wait_ge(s["a_free"], NTOK + 2)
            for t in range(NTOK):
                ins = pe.matmul(PJ[:, t * E:t * E + E], F_hT[0:HID, t, :], F_gw2T[0:HID, :], start=True, stop=True)
            ins.then_inc(s["gates"], 1)
            pe.wait_ge(s["oh"], 1)
            for t in range(NTOK):
                ins = pe.matmul(PV[:, 0:2 * E], ones[:, :], F_oh[:, t, :, :].rearrange("p k e -> p (k e)"),
                                start=(t == 0), stop=(t == NTOK - 1))
            ins.then_inc(s["cnt"], 1)
            pe.wait_ge(s["t_ready"], 1)
            for c in range(4):
                slot = tr_slot()
                for t in range(4 * c, 4 * c + 4):
                    ins = pe.transpose(slot[:, (t % 4) * P:(t % 4 + 1) * P], F_tmp[:, t, :], ident[:, :])
                tr.mark(ins)
            pe.wait_ge(s["m_free"], NTOK + 2)
            for t in range(NTOK):
                if t % 4 == 0:
                    pe.wait_ge(s["tr_free"], tr.base + (tr.n - 4 + t // 4 + 1 + 2))
                if t >= 2:
                    pe.wait_ge(s["l_done"], t - 1)
                for c in range(2):
                    ins = pe.matmul(S_ring[:, t % 2, c * 512:c * 512 + 512], F_tT[:, t, :],
                                    F_B[:, c * 512:c * 512 + 512], start=True, stop=True)
                ins.then_inc(s["l_full"], 1)

        def ffn_scalar(act, F):
            s = F["s"]
            tr = Tally(s["tr_free"])
            act.sem_inc(s["tr_free"], 2)
            act.sem_inc(s["a_free"], 2)

            def tr_out(dst, cols=512, parts=P, n=P):
                act.wait_ge(s["tr_full"], tr.base + (tr.n + 1))
                tr.mark(act.copy(dst, TR_ring[0:parts, tr.n % 2, 0:cols].rearrange("p (c n) -> p c n", n=n)))

            for ro in range(KT):
                for k in range(2):
                    tr_out(FW[:, 4 * k:4 * k + 4, ro * P:ro * P + P])
            for k in range(2):
                tr_out(FW[:, 4 * k:4 * k + 4, DM:DM + HID], cols=4 * HID, n=HID)
            act.wait_ge(s["ln_var"], 1)
            act.activation(f_sd, f_ve, ACT.Sqrt).then_inc(s["ln_sd"], 1)
            with act.Fori(0, NTOK // 2) as tp:
                tr.at(tp * 4 + T_W)
                for q in range(2):
                    for k in range(2):
                        act.wait_ge(s["tr_full"], tr.base + (tr.n + 1))
                        tr.mark(act.copy(F_xT[:, q, 4 * k:4 * k + 4, :],
                                           TR_ring[:, tr.n % 2, :].rearrange("p (c n) -> p c n", n=P)))
                    aux = (PJ, PV)[q]
                    act.wait_ge(s["a_full"], tp * 2 + (q + 1))
                    act.copy(F_h[:, tp * 2 + q, :], aux[:, 0:HID]).then_inc(s["h_in"], 1)
                    act.copy(F_tmp[:, tp * 2 + q, :], aux[:, HID:HID + E * R]).then_inc(s["a_free"], 1)
            tr.at(4 * (NTOK // 2) + T_W)

            def tr_out2(dst, parts=P):
                act.wait_ge(s["tr_full"], tr.base + (tr.n + 1))
                tr.mark(act.copy(dst, TR_ring[0:parts, tr.n % 2, :].rearrange("p (c n) -> p c n", n=P)))

            act.wait_ge(s["h_ln"], 1)
            act.activation(F_vb, F_va, ACT.Sqrt).then_inc(s["h_sd"], 1)
            for c in range(4):
                tr_out2(F_hT[0:HID, 4 * c:4 * c + 4, :], parts=HID)
            act.wait_ge(s["exp_in"], 1)
            act.activation(F_p[:, :, 1], F_p[:, :, 0], ACT.Exp).then_inc(s["exp_out"], 1)
            for c in range(4):
                tr_out2(F_tT[:, 4 * c:4 * c + 4, :])

        def ffn_vector(dve, F):
            s = F["s"]
            ch = Tally(s["chain"])
            dve.sem_inc(s["m_free"], 2)

            def step(ins):
                ch.mark(ins)
                ch.reached(dve)

            for t in range(NTOK):
                if t % 4 == 0:
                    dve.wait_ge(s["x"][t // 4], s["x0"] + 64)
                if t:
                    ch.reached(dve)
                ch.mark(dve.bn_stats(f_st[:, 0, :], FX[:, t, 0:512]))
                step(dve.bn_stats(f_st[:, 1, :], FX[:, t, 512:1024]))
                ch.mark(dve.bn_aggr(f_mv[:, t, :], f_st))
            ch.reached(dve)
            dve.tensor_scalar(f_ve, f_mv[:, :, 1], LN_EPS, None, ALU.add).then_inc(s["ln_var"], 1)

            def inv_sqrt(r, sd, ve, tt):
                step(dve.reciprocal(r, sd))
                step(dve.tensor_tensor(tt, ve, r, ALU.mult))
                step(dve.tensor_tensor(tt, tt, r, ALU.mult))
                step(dve.tensor_scalar(tt, tt, -0.5, 1.5, ALU.mult, ALU.add))
                step(dve.tensor_tensor(r, r, tt, ALU.mult))

            dve.wait_ge(s["ln_sd"], 1)
            inv_sqrt(f_r, f_sd, f_ve, f_t)

            def norm(t, q):
                dve.tensor_scalar(F_xn[:, q, :], FX[:, t, :], f_mv[:, bass.ds(t, 1), 0], f_r[:, bass.ds(t, 1)],
                                  ALU.subtract, ALU.mult).then_inc(s["x_norm"], 1)

            norm(0, 0)
            norm(1, 1)
            CT = ch.n
            for tp in range(NTOK // 2):
                for q in range(2):
                    t = 2 * tp + q
                    dve.wait_ge(s["m_full"], t + 1)
                    if t + 2 < NTOK:
                        norm(t + 2, q)
                    dve.tensor_tensor(FX[:, t, :], FX[:, t, :], S_ring[:, q, :], ALU.add).then_inc(s["m_free"], 1)

            dve.wait_ge(s["h_in"], NTOK)
            dve.wait_ge(s["misc"], 16 * N_MISC)

            def row(k, w=HID):
                return F_row[:, k, 0:w].unsqueeze(1).to_broadcast([P, NTOK, w])

            def col(a, w):
                return a.unsqueeze(2).to_broadcast([P, NTOK, w])

            step(dve.tensor_tensor(F_h, F_h, row(0), ALU.add))
            step(dve.tensor_reduce(F_mu, F_h, mybir.AxisListType.X, ALU.add))
            step(dve.tensor_scalar(F_mu, F_mu, 1.0 / HID, None, ALU.mult))
            step(dve.tensor_tensor(F_h, F_h, col(F_mu, HID), ALU.subtract))
            step(dve.tensor_tensor(F_h2, F_h, F_h, ALU.mult))
            step(dve.tensor_reduce(F_va, F_h2, mybir.AxisListType.X, ALU.add))
            dve.tensor_scalar(F_va, F_va, 1.0 / HID, LN_EPS, ALU.mult, ALU.add).then_inc(s["h_ln"], 1)
            dve.wait_ge(s["h_sd"], 1)
            inv_sqrt(F_mu, F_vb, F_va, F_p[:, :, 0])
            step(dve.tensor_tensor(F_h, F_h, col(F_mu, HID), ALU.mult))
            step(dve.tensor_tensor(F_h, F_h, row(1), ALU.mult))
            step(dve.tensor_tensor(F_h, F_h, row(2), ALU.add))
            dve.tensor_scalar(F_h, F_h, 0.0, None, ALU.max).then_inc(s["h_ready"], 1)
            dve.wait_ge(s["gates"], 1)
            step(dve.tensor_tensor(F_g, PJ[:, 0:NTOK * E].rearrange("p (t e) -> p t e", e=E), row(3, E), ALU.add))
            for t in range(NTOK):
                ch.mark(dve.max(F_top[:, t, :], F_g[:, t, :]))
            ch.reached(dve)
            for t in range(NTOK):
                ch.mark(dve.max_index(F_idx[:, t, :].bitcast(U32), F_top[:, t, :], F_g[:, t, :]))
            ch.reached(dve)
            step(dve.tensor_copy(F_w2, F_idx.bitcast(U32)))
            for k in range(2):
                ch.mark(dve.tensor_tensor(F_oh[:, :, k, :], iota[:, :].unsqueeze(1).to_broadcast([P, NTOK, E]),
                                            col(F_w2[:, :, k], E), ALU.is_equal))
            ch.reached(dve)
            dve.tensor_tensor(F_p[:, :, 0], F_top[:, :, 1], F_top[:, :, 0], ALU.subtract).then_inc(s["exp_in"], 1)
            dve.drain().then_inc(s["oh"], 1)
            dve.wait_ge(s["exp_out"], 1)
            step(dve.tensor_scalar(F_p[:, :, 2], F_p[:, :, 1], 1.0, None, ALU.add))
            step(dve.reciprocal(F_p[:, :, 3], F_p[:, :, 2]))
            step(dve.tensor_scalar(F_p[:, :, 2], F_p[:, :, 3], 1.0 / R, None, ALU.mult))
            step(dve.tensor_tensor(F_p[:, :, 3], F_p[:, :, 2], F_p[:, :, 1], ALU.mult))
            dve.wait_ge(s["cnt"], 1)
            step(dve.tensor_scalar(F_cnt, PV[:, 0:2 * E], float(CAPACITY), None, ALU.is_le))
            for k, dst in enumerate((F_w, F_w2)):
                allowed = F_cnt[:, k * E:k * E + E].unsqueeze(1).to_broadcast([P, NTOK, E])
                step(dve.tensor_tensor(dst, F_oh[:, :, k, :], allowed, ALU.mult))
                step(dve.tensor_tensor(dst, dst, col(F_p[:, :, 2 + k], E), ALU.mult))
            step(dve.tensor_tensor(F_w, F_w, F_w2, ALU.add))
            tmp = F_tmp.rearrange("p t (e r) -> p (t e) r", r=R)
            w = F_w.rearrange("p t e -> p (t e)").unsqueeze(2).to_broadcast([P, NTOK * E, R])
            dve.wait_ge(s["a_free"], NTOK + 2)
            dve.tensor_tensor(tmp, tmp, w, ALU.mult).then_inc(s["t_ready"], 1)
            for t in range(NTOK):
                dve.wait_ge(s["l_full"], t + 1)
                dve.tensor_tensor(FX[:, t, :], FX[:, t, :], S_ring[:, t % 2, :], ALU.add).then_inc(s["l_done"], 1)

        block = ctx.enter_context(nc.Block())

        @block.sync
        def _(sp):
            sp.dma_start(ident[:, :], ident_d).then_inc(s0["const"], 16)
            sp.dma_start(ones[:, :], future_d).then_inc(s0["const"], 16)
            sp.dma_start(iota[:, :], iota_d).then_inc(s0["const"], 16)
            att_sync(sp, A)
            ffn_sync(sp, F1)
            att_sync(sp, B)
            ffn_sync(sp, F2)

        @block.tensor
        def _(pe):
            pe.wait_ge(s0["const"], 48)
            pe.wait_ge(s0["ones"], 4)
            att_tensor(pe, A)
            ffn_tensor(pe, F1)
            att_tensor(pe, B)
            ffn_tensor(pe, F2)

        @block.scalar
        def _(act):
            act.wait_ge(s0["ones"], 4)
            att_scalar(act, A)
            ffn_scalar(act, F1)
            att_scalar(act, B)
            ffn_scalar(act, F2)

        @block.vector
        def _(dve):
            dve.wait_ge(s0["const"], 48)
            dve.tensor_copy(ident16[:, :], ident[:, :]).then_inc(s0["ones"], 1)
            dve.tensor_copy(future16[:, :], ones[:, :]).then_inc(s0["ones"], 1)
            dve.wait_ge(s0["ones"], 2)
            dve.memset(halves[:, :], 0.5).then_inc(s0["ones"], 1)
            dve.memset(ones[:, :], 1.0).then_inc(s0["ones"], 1)
            dve.wait_ge(A["s"]["tab"], 48)
            att_vector(dve, A)
            ffn_vector(dve, F1)
            att_vector(dve, B)
            ffn_vector(dve, F2)

        @block.gpsimd
        def _(pool):
            pool.wait_ge(s0["ones"], 4)
            att_pool(pool, A)
            att_pool(pool, B)


_INS = ["L0_attn_a_hidden_states", "L0_attn_a_Wq", "L0_attn_a_Wk", "L0_attn_a_Wv", "L0_attn_a_Wo",
        "L0_attn_b_Wq", "L0_attn_b_bq", "L0_attn_b_Wk", "L0_attn_b_bk", "L0_attn_b_Wv", "L0_attn_b_bv",
        "L0_attn_b_Wo", "L0_attn_b_bo", "L0_ffn_weight", "L0_ffn_lora_A", "L0_ffn_lora_B", "L0_ffn_gw1",
        "L0_ffn_gb1", "L0_ffn_ln_gamma", "L0_ffn_ln_beta", "L0_ffn_gw2", "L0_ffn_gb2"]


def tables():
    pos = np.arange(SEQ, dtype=np.float32)
    inv = (1.0 / np.power(np.float32(10000.0), np.arange(0, HD, 2, dtype=np.float32) / np.float32(HD))).astype(np.float32)
    ang = (pos[None, :] * inv[:, None]).astype(np.float32)
    cos, sin = np.cos(ang).astype(np.float32), np.sin(ang).astype(np.float32)
    d = np.arange(HD)
    half, pairs = d % (HD // 2), d // 2
    sign_half = np.where(d < HD // 2, -1.0, 1.0).astype(np.float32)
    sign_pairs = np.where(d % 2 == 0, -1.0, 1.0).astype(np.float32)
    c = np.stack([np.tile(cos[half], (HG, 1)), np.tile(cos[pairs], (HG, 1))])
    s = np.stack([np.tile(sin[half] * sign_half[:, None], (HG, 1)), np.tile(sin[pairs] * sign_pairs[:, None], (HG, 1))])
    k = np.float32(QK_SCALE)
    future = np.where(np.arange(P)[None, :] > np.arange(P)[:, None], FUTURE, 0.0)
    x = np.linspace(-8.0, 8.0, 16001)
    cdf = np.cumsum(np.exp(-x * x / 2))
    keys = np.maximum(np.arange(NT)[None, :] * P + np.arange(P)[:, None] + 1, P + 1)
    z = np.interp(1.0 - AIM / keys, cdf / cdf[-1], x)
    slope = 1.0 / (keys * np.exp(-z * z / 2) / np.sqrt(2 * np.pi))
    return {
        "rope_cos": (c * k).astype(np.float32), "rope_sin": (s * k).astype(np.float32),
        "ident": np.eye(P, dtype=np.float32),
        "future": future.astype(np.float32),
        "expert_ids": np.tile(np.arange(E, dtype=np.float32), (P, 1)),
        "search": np.concatenate([z, slope], axis=1).astype(np.float32),
    }


def kernel(**inputs):
    import numpy as _np
    import concourse.bacc as _bacc
    from concourse import mybir as _mybir
    from concourse.bass_utils import run_bass_kernel_spmd as _run

    nc = _bacc.Bacc("TRN2", target_bir_lowering=False, num_devices=1)
    arrays, named = {}, {}
    for name in _INS:
        a = _np.ascontiguousarray(inputs[name])
        arrays[f"in_{name}"] = a
        named[name] = nc.dram_tensor(f"in_{name}", a.shape, _mybir.dt.from_np(a.dtype), kind="ExternalInput").ap()
    consts = []
    for name, a in tables().items():
        arrays[f"const_{name}"] = a
        consts.append(nc.dram_tensor(f"const_{name}", a.shape, _mybir.dt.from_np(a.dtype), kind="ExternalInput").ap())
    scratch = [nc.dram_tensor(f"x{k}", (BATCH * SEQ, DM), _mybir.dt.float32, kind="Internal").ap() for k in (1, 2, 3)]
    out = nc.dram_tensor("out", (BATCH, SEQ, DM), _mybir.dt.float32, kind="ExternalOutput").ap()
    build(nc, named, *consts, *scratch, out)
    r = _run(nc, [arrays], core_ids=[0])
    return r.results[0]["out"]
```
